# Optimizing a Trainium2 kernel written in Bass

```python
import numpy as np
import jax
import jax.numpy as jnp

def _softmax(x, axis=-1):
    return jax.nn.softmax(x, axis=axis)

def _gelu(x):
    return jax.nn.gelu(x, approximate=True)

def _silu(x):
    return jax.nn.silu(x)

def _sigmoid(x):
    return jax.nn.sigmoid(x)

def _layernorm(x, axis=-1, eps=1e-05):
    m = jnp.mean(x, axis=axis, keepdims=True)
    v = jnp.var(x, axis=axis, keepdims=True)
    return (x - m) / jnp.sqrt(v + eps)

def _scatter_add(tgt, idx, src, axis=0):
    return tgt.at[idx].add(src)

def _segment_sum(src, seg, n):
    return jax.ops.segment_sum(src, seg, n)
kernel_name = 'mk_conv_preact_d2_conv_nchw512_r4_eeacac'

def setup_inputs(seed: int=0):
    np.random.seed(seed)
    _w = jnp.asarray

    def _rec_inputs():
        import jax
        import jax.numpy as jnp
        _gk = jax.random.key(seed)
        x = -0.0003929 + 0.9999 * jax.random.normal(jax.random.fold_in(_gk, 1), (8, 128, 16, 16), jnp.float32)
        return x
    x = _rec_inputs()

    def _L0_conv_setup():
        import jax, jax.numpy as jnp
        import numpy as np
        import math
        B, C, H, W, S = (8, 128, 16, 16, 4)
        key = jax.random.key(seed)
        ks = jax.random.split(key, 7)
        s = 1.0 / math.sqrt(C)
        x = jax.random.normal(ks[0], (B, C, H, W), jnp.float32)
        Wq = jax.random.uniform(ks[1], (C, C), jnp.float32, -s, s)
        bq = jax.random.uniform(ks[2], (C,), jnp.float32, -s, s)
        Wk = jax.random.uniform(ks[3], (C, C), jnp.float32, -s, s)
        bk = jax.random.uniform(ks[4], (C,), jnp.float32, -s, s)
        Wv = jax.random.uniform(ks[5], (C, C), jnp.float32, -s, s)
        bv = jax.random.uniform(ks[6], (C,), jnp.float32, -s, s)
        return {'x': x, 'Wq': Wq, 'bq': bq, 'Wk': Wk, 'bk': bk, 'Wv': Wv, 'bv': bv}
    _L0_conv_all = _L0_conv_setup()
    _L0_conv_in = {k: v for k, v in _L0_conv_all.items() if k in ('Wq', 'bq', 'Wk', 'bk', 'Wv', 'bv')}
    del _L0_conv_all

    def _L1_conv_setup():
        import jax, jax.numpy as jnp
        import numpy as np
        from jax import lax
        DIM = 128
        ORDER = 3
        DIMS = [DIM // 2 ** i for i in range(ORDER)][::-1]
        SUMD = sum(DIMS)
        SCALE = 1.0

        def conv1x1(x, w, b):
            return jnp.einsum('oc,bchw->bohw', w, x) + b[None, :, None, None]

        def dwconv7(x, w, b):
            y = lax.conv_general_dilated(x, w, window_strides=(1, 1), padding=((3, 3), (3, 3)), dimension_numbers=('NCHW', 'OIHW', 'NCHW'), feature_group_count=x.shape[1])
            return y + b[None, :, None, None]
        key = jax.random.key(seed)
        ks = jax.random.split(key, 12)
        s = 0.02
        return {'x': jax.random.normal(ks[0], (4, DIM, 32, 32), jnp.float32), 'w_in': jax.random.normal(ks[1], (2 * DIM, DIM), jnp.float32) * s, 'b_in': jnp.zeros((2 * DIM,), jnp.float32), 'dw_w': jax.random.normal(ks[2], (SUMD, 1, 7, 7), jnp.float32) * s, 'dw_b': jnp.zeros((SUMD,), jnp.float32), 'pw0_w': jax.random.normal(ks[3], (DIMS[1], DIMS[0]), jnp.float32) * s, 'pw0_b': jnp.zeros((DIMS[1],), jnp.float32), 'pw1_w': jax.random.normal(ks[4], (DIMS[2], DIMS[1]), jnp.float32) * s, 'pw1_b': jnp.zeros((DIMS[2],), jnp.float32), 'w_out': jax.random.normal(ks[5], (DIM, DIM), jnp.float32) * s, 'b_out': jnp.zeros((DIM,), jnp.float32)}
    _L1_conv_all = _L1_conv_setup()
    _L1_conv_in = {k: v for k, v in _L1_conv_all.items() if k in ('w_in', 'b_in', 'dw_w', 'dw_b', 'pw0_w', 'pw0_b', 'pw1_w', 'pw1_b', 'w_out', 'b_out')}
    del _L1_conv_all
    return {'x': x, 'L0_conv_Wq': _L0_conv_in['Wq'], 'L0_conv_bq': _L0_conv_in['bq'], 'L0_conv_Wk': _L0_conv_in['Wk'], 'L0_conv_bk': _L0_conv_in['bk'], 'L0_conv_Wv': _L0_conv_in['Wv'], 'L0_conv_bv': _L0_conv_in['bv'], 'L1_conv_w_in': _L1_conv_in['w_in'], 'L1_conv_b_in': _L1_conv_in['b_in'], 'L1_conv_dw_w': _L1_conv_in['dw_w'], 'L1_conv_dw_b': _L1_conv_in['dw_b'], 'L1_conv_pw0_w': _L1_conv_in['pw0_w'], 'L1_conv_pw0_b': _L1_conv_in['pw0_b'], 'L1_conv_pw1_w': _L1_conv_in['pw1_w'], 'L1_conv_pw1_b': _L1_conv_in['pw1_b'], 'L1_conv_w_out': _L1_conv_in['w_out'], 'L1_conv_b_out': _L1_conv_in['b_out']}

def reference(x, L0_conv_Wq, L0_conv_bq, L0_conv_Wk, L0_conv_bk, L0_conv_Wv, L0_conv_bv, L1_conv_w_in, L1_conv_b_in, L1_conv_dw_w, L1_conv_dw_b, L1_conv_pw0_w, L1_conv_pw0_b, L1_conv_pw1_w, L1_conv_pw1_b, L1_conv_w_out, L1_conv_b_out):
    import jax
    import jax.numpy as jnp

    def _L0_conv_ref(x, Wq, bq, Wk, bk, Wv, bv):
        import jax, jax.numpy as jnp
        import numpy as np
        import math
        B, C, H, W, S = (8, 128, 16, 16, 4)
        b, c, h, w = x.shape
        nb = h // S * (w // S)
        hw = h * w
        ss = S * S
        x_avg = x.reshape(b, c, h // S, S, w // S, S).mean(axis=(3, 5))
        x_avg = x_avg.reshape(b, c, nb).transpose(0, 2, 1)
        Q = x_avg @ Wq.T + bq
        K = x_avg @ Wk.T + bk
        A = jax.nn.softmax(jnp.einsum('bnc,bmc->bnm', Q, K) / jnp.sqrt(jnp.float32(c)), axis=-1)
        x_flat = x.reshape(b, c, hw).transpose(0, 2, 1)
        V = x_flat @ Wv.T + bv
        Vsum = V.reshape(b, hw // ss, ss, c).sum(axis=2)
        out_small = jnp.einsum('bnm,bmc->bnc', A, Vsum)
        out_flat = jnp.repeat(out_small, ss, axis=1)
        return out_flat.transpose(0, 2, 1).reshape(b, c, h, w)

    def _L1_conv_ref(x, w_in, b_in, dw_w, dw_b, pw0_w, pw0_b, pw1_w, pw1_b, w_out, b_out):
        import jax, jax.numpy as jnp
        import numpy as np
        from jax import lax
        DIM = 128
        ORDER = 3
        DIMS = [DIM // 2 ** i for i in range(ORDER)][::-1]
        SUMD = sum(DIMS)
        SCALE = 1.0

        def conv1x1(x, w, b):
            return jnp.einsum('oc,bchw->bohw', w, x) + b[None, :, None, None]

        def dwconv7(x, w, b):
            y = lax.conv_general_dilated(x, w, window_strides=(1, 1), padding=((3, 3), (3, 3)), dimension_numbers=('NCHW', 'OIHW', 'NCHW'), feature_group_count=x.shape[1])
            return y + b[None, :, None, None]
        fused = conv1x1(x, w_in, b_in)
        pwa = fused[:, :DIMS[0]]
        abc = fused[:, DIMS[0]:]
        dw_abc = dwconv7(abc, dw_w, dw_b) * SCALE
        dw0 = dw_abc[:, :DIMS[0]]
        dw1 = dw_abc[:, DIMS[0]:DIMS[0] + DIMS[1]]
        dw2 = dw_abc[:, DIMS[0] + DIMS[1]:]
        h = pwa * dw0
        h = conv1x1(h, pw0_w, pw0_b) * dw1
        h = conv1x1(h, pw1_w, pw1_b) * dw2
        return conv1x1(h, w_out, b_out)

    def _gn(v, G=32, eps=1e-05):
        B_, C_, H_, W_ = v.shape
        g = v.reshape(B_, G, C_ // G, H_, W_)
        m = jnp.mean(g, axis=(2, 3, 4), keepdims=True)
        s = jnp.var(g, axis=(2, 3, 4), keepdims=True)
        return ((g - m) / jnp.sqrt(s + eps)).reshape(v.shape)

    def _ln_c(v, eps=1e-06):
        m = jnp.mean(v, axis=1, keepdims=True)
        s = jnp.var(v, axis=1, keepdims=True)
        return (v - m) / jnp.sqrt(s + eps)

    def _ln_t(v, eps=1e-05):
        m = jnp.mean(v, axis=-1, keepdims=True)
        s = jnp.var(v, axis=-1, keepdims=True)
        return (v - m) / jnp.sqrt(s + eps)

    def _to_tokens(v):
        B_, C_, H_, W_ = v.shape
        return v.reshape(B_, C_, H_ * W_).transpose(0, 2, 1)

    def _from_tokens(t, like):
        B_, C_, H_, W_ = like.shape
        return t.transpose(0, 2, 1).reshape(B_, C_, H_, W_)
    x = x + _L0_conv_ref(_gn(x), L0_conv_Wq, L0_conv_bq, L0_conv_Wk, L0_conv_bk, L0_conv_Wv, L0_conv_bv)
    x = x + _L1_conv_ref(_gn(x), L1_conv_w_in, L1_conv_b_in, L1_conv_dw_w, L1_conv_dw_b, L1_conv_pw0_w, L1_conv_pw0_b, L1_conv_pw1_w, L1_conv_pw1_b, L1_conv_w_out, L1_conv_b_out)
    return x

_drawn_inputs = setup_inputs


def setup_inputs(seed=0):
    import zlib

    import numpy as np

    out = dict(_drawn_inputs(seed))
    spreads = {'L1_conv_b_in': (0.0, 0.8),
     'L1_conv_dw_b': (0.0, 0.8),
     'L1_conv_pw0_b': (0.0, 0.8),
     'L1_conv_pw1_b': (0.0, 0.8),
     'L1_conv_b_out': (0.0, 2.0)}
    factors = {'L0_conv_Wq': 6.953,
     'L0_conv_bq': 8.0,
     'L0_conv_Wk': 6.5,
     'L0_conv_bk': 200.0,
     'L1_conv_w_in': 8.0,
     'L1_conv_dw_w': 8.0,
     'L1_conv_pw0_w': 8.0,
     'L1_conv_pw1_w': 8.0,
     'L1_conv_w_out': 8.0}
    for name, (base, spread) in spreads.items():
        noise = np.random.default_rng([zlib.crc32(name.encode()), seed]).standard_normal(out[name].shape)
        drawn = base * np.exp(spread * noise) if base else spread * noise
        out[name] = jnp.asarray(drawn.astype(out[name].dtype))
    for name, factor in factors.items():
        out[name] = (out[name] * factor).astype(out[name].dtype)
    return out
```

```python
from contextlib import ExitStack

import concourse.bass as bass
from concourse import mybir

F32 = mybir.dt.float32
ALU = mybir.AluOpType
ACT = mybir.ActivationFunctionType
AX_X = mybir.AxisListType.X

C = 128
B, H, W = 8, 16, 16
HW = H * W
NTOK = B * HW
S = 4
GN = 4
K = 7
PAD = K // 2
GC = C // H
PITCH = W + PAD
ROW = 160
BW = B * W
CH = 512
NCH = NTOK // CH
IPC = CH // HW
QUAD = 4
TQ = 3
EPS = 1e-5
OFF_BLOCK = -1e30

DIMS = (C // 4, C // 2, C)
NGR = [d // GC for d in DIMS]
G0 = [0, NGR[0], NGR[0] + NGR[1]]
NG = sum(NGR)
NQ = NG // QUAD

EARLY = [("gavg", C), ("wq", C), ("wk", C), ("wv", C), ("ident", C), ("offmask", C), ("blk", GC),
         ("bq", 1), ("bk", 1), ("bv", 1), ("b_inA", 1), ("b_inB", 1), ("pw0_b", 1), ("pw1_b", 1),
         ("b_out", 1), ("dw_b", NG)]
LATE = [("w_in", 2 * C), ("pw0", DIMS[1]), ("pw1", C), ("w_out", C)]


def columns(layout):
    at, out = 0, {}
    for name, n in layout:
        out[name] = (at, at + n)
        at += n
    return out, at


E_COL, E_N = columns(EARLY)
L_COL, L_N = columns(LATE)


def build(nc, x, early, late, taps, out):
    with ExitStack() as ctx:
        def sb(name, shape):
            return ctx.enter_context(nc.sbuf_tensor(name, shape, F32))

        def sem(name):
            return ctx.enter_context(nc.semaphore(name))

        x_sb = sb("x_sb", [C, B, H, W])
        x1 = sb("x1", [C, B, H, W])
        x1n = sb("x1n", [C, B, HW])
        e_sb = sb("e_sb", [C, E_N])
        l_sb = sb("l_sb", [C, L_N])
        taps_sb = sb("taps_sb", [C, NG, K, H])
        toep = sb("toep", [C, TQ * QUAD, K, GC, H])
        abcA = sb("abcA", [C, H, ROW])
        abcB = sb("abcB", [C, H, ROW])
        cin = sb("cin", [C, NG, ROW])
        cout = sb("cout", [C, NG, BW])
        dw = [sb(f"dw{i}", [C, H, BW]) for i in range(3)]
        h0 = sb("h0", [DIMS[0], H, BW])
        h1 = sb("h1", [DIMS[1], H, BW])
        h2 = x1n[:, :, :].rearrange("p b n -> p (b n)").rearrange("p (h n) -> p h n", h=H)
        y_sb = sb("y_sb", [C, B, H, W])

        st = sb("st", [C, B, 6])
        colsum = sb("colsum", [C, B, H, S])
        sums = sb("sums", [C, 2, B, H])
        dev = sb("dev", [C, B, 2])
        dev2 = sb("dev2", [C, B, 2])
        vpart = sb("vpart", [C, B, 2])
        veps = sb("veps", [C, B])
        power = sb("power", [C, B])
        a1 = sb("a1", [C, B])
        b1 = sb("b1", [C, B])
        scaled = sb("scaled", [C, 2, B, H])
        normed = sb("normed", [C, 2, B, H])
        q_sb = sb("q_sb", [C, C])
        k_sb = sb("k_sb", [C, C])
        v_sb = sb("v_sb", [C, C])
        score = sb("score", [C, C])
        nmax = sb("nmax", [C, 1])
        probs = sb("probs", [C, C])
        rsum = sb("rsum", [C, 1])
        rinv = sb("rinv", [C, 1])
        pnorm = sb("pnorm", [C, C])
        pT = sb("pT", [C, C])
        o_sb = sb("o_sb", [C, B, H])
        mdiff = sb("mdiff", [C, B])
        msum = sb("msum", [C, B])
        m2 = sb("m2", [C, B])
        rcen = sb("rcen", [C, B, H])
        rsq = sb("rsq", [C, B])
        within = sb("within", [C, B])
        yrow = sb("yrow", [C, B, H])
        ysum = sb("ysum", [C, B])
        yd = sb("yd", [C, B, H])
        yd2 = sb("yd2", [C, B, H])
        yq = sb("yq", [C, B])
        v2 = sb("v2", [C, B])
        veps2 = sb("veps2", [C, B])
        a2 = sb("a2", [C, B])
        b2 = sb("b2", [C, B])

        bank = [ctx.enter_context(nc.psum_tensor(f"bank{i}", [C, CH], F32)) for i in range(8)]
        conv_bank = [bank[4], bank[5], bank[6]]
        psM, psV = bank[6], bank[7]
        psQ, psK, psVt, psS = bank[0], bank[1], bank[2], bank[3]
        psP, psO = bank[4], bank[5]

        def ecol(name, rows=C):
            a, b = E_COL[name]
            return e_sb[0:rows, a:b]

        def lcol(name, rows=C):
            a, b = L_COL[name]
            return l_sb[0:rows, a:b]

        x_in = [sem(f"x_in{i}") for i in range(NCH)]
        early_in, late_in = sem("early_in"), sem("late_in")
        taps_in = [sem(f"taps_in{i}") for i in range(3)]
        consts = sem("consts")
        stats_done, mean_ps, vpart_done, var_ps = sem("stats_done"), sem("mean_ps"), sem("vpart_done"), sem("var_ps")
        veps_done, rstd_done = sem("veps_done"), sem("rstd_done")
        normed_done, qk_ps, v_ps, q_done, k_done, v_done = (
            sem("normed_done"), sem("qk_ps"), sem("v_ps"), sem("q_done"), sem("k_done"), sem("v_done"))
        score_ps, score_done, exp_done, pnorm_done = sem("score_ps"), sem("score_done"), sem("exp_done"), sem("pnorm_done")
        pT_ps, pT_done, o_ps = sem("pT_ps"), sem("pT_done"), sem("o_ps")
        ysum_done, mean2_ps, v2_done, var2_ps = sem("ysum_done"), sem("mean2_ps"), sem("v2_done"), sem("var2_ps")
        veps2_done, rstd2_done = sem("veps2_done"), sem("rstd2_done")
        affine_done = sem("affine_done")
        x1n_dve, x1n_act = sem("x1n_dve"), sem("x1n_act")
        inA_ps, inB_ps, inA_done, inB_done = sem("inA_ps"), sem("inB_ps"), sem("inA_done"), sem("inB_done")
        toep_done = sem("toep_done")
        cin_in = [sem(f"cin_in{g}") for g in range(NG)]
        conv_ps, conv_done = sem("conv_ps"), sem("conv_done")
        dw_in = [sem(f"dw_in{i}") for i in range(3)]
        h0_done, pw0_ps, h1_done, pw1_ps, h2_done, out_ps, y_done, xb_done = (
            sem("h0_done"), sem("pw0_ps"), sem("h1_done"), sem("pw1_ps"), sem("h2_done"), sem("out_ps"),
            sem("y_done"), sem("xb_done"))
        stored = sem("stored")
        dve_step = sem("dve_step")
        pads_done = sem("pads_done")

        ACT_IMAGES = (3, 5, 7)
        x1n_need = []
        for k in range(NCH):
            upto = range((k + 1) * IPC)
            x1n_need.append((len([b for b in upto if b not in ACT_IMAGES]), len([b for b in upto if b in ACT_IMAGES])))

        def inner(t):
            return t[:, :, PAD:PAD + B * PITCH].rearrange("p h (b s) -> p b h s", s=PITCH)[:, :, :, 0:W]

        def pair(t, k):
            return t[:, :, k * IPC * W:(k + 1) * IPC * W]

        block = ctx.enter_context(nc.Block())

        @block.sync
        def _(sp):
            for k in range(NCH):
                sp.dma_start(x_sb[:, k * IPC:(k + 1) * IPC, :, :].rearrange("c b h w -> c b (h w)"),
                             x[k * IPC:(k + 1) * IPC].rearrange("b c h w -> c b (h w)")).then_inc(x_in[k], 16)
            for s in range(3):
                sp.dma_start(taps_sb[:, G0[s]:G0[s] + NGR[s]], taps[:, G0[s]:G0[s] + NGR[s]]).then_inc(taps_in[s], 16)
            sp.dma_start(l_sb[:, :], late).then_inc(late_in, 16)
            sp.wait_ge(pads_done, 1)
            for s, (tile, base, ready) in enumerate(((abcA, DIMS[0], inA_done), (abcA, 2 * DIMS[0], inA_done),
                                                     (abcB, 0, inB_done))):
                sp.wait_ge(ready, NCH)
                for j in range(NGR[s]):
                    g = G0[s] + j
                    sp.dma_start(cin[:, g, :], tile[base + j:base + j + NGR[s] * (GC - 1) + 1:NGR[s], :, :]
                                 ).then_inc(cin_in[g], 16)
            for s in range(3):
                for j in range(NGR[s]):
                    g = G0[s] + j
                    sp.wait_ge(conv_done, g + 1)
                    sp.dma_start(dw[s][j:j + NGR[s] * (GC - 1) + 1:NGR[s], :, :], cout[:, g, :]
                                 ).then_inc(dw_in[s], 16)
            for k in range(NCH):
                sp.wait_ge(y_done, k + 1)
                sp.dma_start(out[k * IPC:(k + 1) * IPC].rearrange("b c h w -> c b (h w)"),
                             y_sb[:, k * IPC:(k + 1) * IPC, :, :].rearrange("c b h w -> c b (h w)")
                             ).then_inc(stored, 16)
            sp.wait_ge(stored, 16 * NCH)

        @block.gpsimd
        def _(pool):
            nc.gpsimd.memset(power[:, :], -0.5).then_inc(consts, 1)
            nc.gpsimd.memset(abcA[:, :, :], 0.0)
            nc.gpsimd.memset(abcB[:, :, :], 0.0).then_inc(pads_done, 1)
            pool.wait_ge(consts, 1)
            pool.wait_ge(veps_done, 1)
            nc.gpsimd.tensor_tensor(a1[:, :], veps[:, :], power[:, :], ALU.pow).then_inc(rstd_done, 1)
            pool.wait_ge(veps2_done, 1)
            nc.gpsimd.tensor_tensor(a2[:, :], veps2[:, :], power[:, :], ALU.pow).then_inc(rstd2_done, 1)
            pool.wait_ge(x1n_dve, B - len(ACT_IMAGES))
            pool.wait_ge(x1n_act, len(ACT_IMAGES))
            nc.gpsimd.tensor_scalar(x1[:, :, :, :], x1[:, :, :, :], ecol("b_out"), 1.0, ALU.add, ALU.mult
                                    ).then_inc(xb_done, 1)

        @block.scalar
        def _(act):
            act.dma_start(e_sb[:, :], early).then_inc(early_in, 16)
            act.wait_ge(early_in, 16)
            act.wait_ge(qk_ps, 1)
            nc.scalar.activation(q_sb[:, :], psQ[:, 0:C], ACT.Identity, bias=ecol("bq")).then_inc(q_done, 1)
            act.wait_ge(v_ps, 1)
            nc.scalar.copy(v_sb[:, :], psVt[:, 0:C]).then_inc(v_done, 1)
            act.wait_ge(score_done, 1)
            nc.scalar.activation(probs[:, :], score[:, :], ACT.Exp, bias=nmax[:, :], accum_out=rsum[:, :]
                                 ).then_inc(exp_done, 1)
            act.wait_ge(affine_done, 1)
            act.wait_ge(rstd2_done, 1)
            for b in ACT_IMAGES:
                nc.scalar.activation(x1n[:, b, :], x1[:, b, :, :].rearrange("p h w -> p (h w)"), ACT.Identity,
                                     bias=b2[:, b:b + 1], scale=a2[:, b:b + 1]).then_inc(x1n_act, 1)
            act.wait_ge(pads_done, 1)
            for k in range(NCH):
                act.wait_ge(inA_ps, k + 1)
                nc.scalar.activation(inner(abcA)[:, k * IPC:(k + 1) * IPC],
                                     bank[k][:, :].rearrange("p (b h w) -> p b h w", b=IPC, h=H),
                                     ACT.Identity, bias=ecol("b_inA")).then_inc(inA_done, 1)
            for g in range(NG):
                act.wait_ge(conv_ps, g + 1)
                nc.scalar.activation(cout[:, g, :], conv_bank[g % 3][:, 0:BW], ACT.Identity,
                                     bias=ecol("dw_b")[:, g:g + 1]).then_inc(conv_done, 1)

        @block.vector
        def _(dve):
            steps = [0]

            def link(ins):
                steps[0] += 1
                ins.then_inc(dve_step, 1)
                dve.wait_ge(dve_step, steps[0])

            todo = [(q, c) for q in range(NQ) for c in range(GC)]

            def matrices(n):
                for _ in range(n):
                    q, c = todo.pop(0)
                    if c == 0:
                        s = max(i for i in range(3) if G0[i] <= q * QUAD)
                        if q * QUAD == G0[s]:
                            dve.wait_ge(taps_in[s], 16)
                        if q >= TQ:
                            dve.wait_ge(conv_ps, (q - TQ + 1) * QUAD)
                    at = q % TQ * QUAD
                    ins = nc.vector.tensor_scalar(
                        toep[:, at:at + QUAD, :, c, :],
                        taps_sb[:, q * QUAD:(q + 1) * QUAD, :, :],
                        ecol("blk")[:, c:c + 1], None, ALU.mult)
                    if c == GC - 1:
                        ins.then_inc(toep_done, 1)

            for k in range(NCH):
                dve.wait_ge(x_in[k], 16)
                im = slice(k * IPC, (k + 1) * IPC)
                for b in range(k * IPC, (k + 1) * IPC):
                    nc.vector.bn_stats(st[:, b, :], x_sb[:, b, :, :].rearrange("p h w -> p (h w)")
                                       ).then_inc(stats_done, 1)
                last = nc.vector.tensor_reduce(
                    colsum[:, im], x_sb[:, im].rearrange("p b h (v s) -> p b h v s", s=S), AX_X, ALU.add)
            link(last)
            nc.vector.tensor_reduce(sums[:, 1, :, :], colsum[:, :, :, :], AX_X, ALU.add)
            link(nc.vector.tensor_reduce(
                sums[:, 0, :, :], colsum[:, :, :, :].rearrange("p b (u s) v -> p (b u) v s", s=S), AX_X, ALU.add))
            dve.wait_ge(mean_ps, 1)
            link(nc.vector.tensor_tensor(dev[:, :, :], st[:, :, 1:6:3],
                                         psM[:, 0:B].unsqueeze(2).to_broadcast([C, B, 2]), ALU.subtract))
            link(nc.vector.tensor_tensor(dev2[:, :, :], dev[:, :, :], dev[:, :, :], ALU.mult))
            nc.vector.scalar_tensor_tensor(vpart[:, :, :], st[:, :, 2:6:3], 2.0 / HW, dev2[:, :, :],
                                           ALU.mult, ALU.add).then_inc(vpart_done, 1)
            dve.wait_ge(var_ps, 1)
            nc.vector.tensor_scalar(veps[:, :], psV[:, 0:B], EPS, None, ALU.add).then_inc(veps_done, 1)
            matrices(4)
            dve.wait_ge(rstd_done, 1)
            nc.vector.tensor_tensor(scaled[:, :, :, :], sums[:, :, :, :],
                                    a1[:, :].unsqueeze(1).unsqueeze(3).to_broadcast([C, 2, B, H]), ALU.mult)
            link(nc.vector.scalar_tensor_tensor(b1[:, :], psM[:, 0:B], -1.0, a1[:, :], ALU.mult, ALU.mult))
            for half in range(2):
                nc.vector.scalar_tensor_tensor(normed[:, half, :, :], scaled[:, half, :, :], 1.0 / H,
                                               b1[:, :].unsqueeze(2).to_broadcast([C, B, H]),
                                               ALU.mult, ALU.add).then_inc(normed_done, 1)
            dve.wait_ge(early_in, 16)
            link(nc.vector.tensor_tensor(mdiff[:, :], st[:, :, 1], st[:, :, 4], ALU.subtract))
            nc.vector.tensor_tensor(msum[:, :], st[:, :, 1], st[:, :, 4], ALU.add)
            nc.vector.tensor_tensor(m2[:, :], st[:, :, 2], st[:, :, 5], ALU.add)
            dve.wait_ge(qk_ps, 2)
            nc.vector.tensor_scalar(k_sb[:, :], psK[:, 0:C], ecol("bk"), None, ALU.add).then_inc(k_done, 1)
            link(nc.vector.tensor_tensor(mdiff[:, :], mdiff[:, :], mdiff[:, :], ALU.mult))
            link(nc.vector.scalar_tensor_tensor(rcen[:, :, :], msum[:, :].unsqueeze(2).to_broadcast([C, B, H]),
                                                -W / 2.0, sums[:, 1, :, :], ALU.mult, ALU.add))
            dve.wait_ge(score_ps, 1)
            link(nc.vector.scalar_tensor_tensor(score[:, :], psS[:, 0:C], float(C) ** -0.5, ecol("offmask"),
                                                ALU.mult, ALU.add))
            nc.vector.tensor_reduce(nmax[:, :], score[:, :], AX_X, ALU.max, negate=True).then_inc(score_done, 1)
            link(nc.vector.scalar_tensor_tensor(m2[:, :], mdiff[:, :], HW / 4.0, m2[:, :], ALU.mult, ALU.add))
            link(nc.vector.tensor_tensor(rcen[:, :, :], rcen[:, :, :], rcen[:, :, :], ALU.mult))
            link(nc.vector.tensor_reduce(rsq[:, :], rcen[:, :, :], AX_X, ALU.add))
            link(nc.vector.scalar_tensor_tensor(within[:, :], rsq[:, :], -1.0 / W, m2[:, :], ALU.mult, ALU.add))
            nc.vector.tensor_scalar(within[:, :], within[:, :], 0.0, None, ALU.max)
            dve.wait_ge(exp_done, 1)
            link(nc.vector.reciprocal(rinv[:, :], rsum[:, :]))
            nc.vector.tensor_scalar(pnorm[:, :], probs[:, :], rinv[:, :], None, ALU.mult).then_inc(pnorm_done, 1)
            matrices(2)
            dve.wait_ge(pT_ps, 1)
            nc.vector.tensor_copy(pT[:, :], psP[:, 0:C]).then_inc(pT_done, 1)
            matrices(2)
            dve.wait_ge(o_ps, 1)
            link(nc.vector.tensor_scalar(o_sb[:, :, :].rearrange("p b h -> p (b h)"), psO[:, 0:C], ecol("bv"),
                                         float(W), ALU.add, ALU.mult))
            link(nc.vector.scalar_tensor_tensor(yrow[:, :, :], sums[:, 1, :, :], 1.0 / W, o_sb[:, :, :],
                                                ALU.mult, ALU.add))
            nc.vector.tensor_reduce(ysum[:, :], yrow[:, :, :], AX_X, ALU.add).then_inc(ysum_done, 1)

            def residual(k):
                im = slice(k * IPC, (k + 1) * IPC)
                return nc.vector.tensor_tensor(
                    x1[:, im].rearrange("p b h w -> p (b h) w"), x_sb[:, im].rearrange("p b h w -> p (b h) w"),
                    o_sb[:, im].rearrange("p b h -> p (b h)").unsqueeze(2).to_broadcast([C, IPC * H, W]), ALU.add)

            residual(0)
            dve.wait_ge(mean2_ps, 1)
            link(nc.vector.scalar_tensor_tensor(yd[:, :, :], psM[:, 0:B].unsqueeze(2).to_broadcast([C, B, H]),
                                                -8.0 / (GN * H), yrow[:, :, :], ALU.mult, ALU.add))
            link(nc.vector.tensor_tensor(yd2[:, :, :], yd[:, :, :], yd[:, :, :], ALU.mult))
            link(nc.vector.tensor_reduce(yq[:, :], yd2[:, :, :], AX_X, ALU.add))
            nc.vector.scalar_tensor_tensor(v2[:, :], yq[:, :], float(W), within[:, :], ALU.mult, ALU.add
                                           ).then_inc(v2_done, 1)
            residual(1)
            dve.wait_ge(var2_ps, 1)
            nc.vector.tensor_scalar(veps2[:, :], psV[:, 0:B], 8.0 / (GN * HW), EPS, ALU.mult, ALU.add
                                    ).then_inc(veps2_done, 1)
            residual(2)
            link(residual(3))
            dve.wait_ge(rstd2_done, 1)
            ins = nc.vector.scalar_tensor_tensor(b2[:, :], psM[:, 0:B], -8.0 / (GN * H), a2[:, :],
                                                 ALU.mult, ALU.mult)
            ins.then_inc(affine_done, 1)
            dve.wait_ge(affine_done, 1)
            for b in range(B):
                if b not in ACT_IMAGES:
                    nc.vector.tensor_scalar(x1n[:, b, :], x1[:, b, :, :].rearrange("p h w -> p (h w)"),
                                            a2[:, b:b + 1], b2[:, b:b + 1], ALU.mult, ALU.add
                                            ).then_inc(x1n_dve, 1)
            matrices(8)
            dve.wait_ge(pads_done, 1)
            for k in range(NCH):
                dve.wait_ge(inB_ps, k + 1)
                nc.vector.tensor_scalar(inner(abcB)[:, k * IPC:(k + 1) * IPC],
                                        bank[k if k < 0 else (4 + k) % 8][:, :].rearrange(
                                            "p (b h w) -> p b h w", b=IPC, h=H),
                                        ecol("b_inB"), None, ALU.add).then_inc(inB_done, 1)
            matrices(8)
            dve.wait_ge(inA_done, NCH)
            dve.wait_ge(dw_in[0], 16 * NGR[0])
            for k in range(NCH):
                nc.vector.tensor_tensor(
                    pair(h0, k).rearrange("p h (b w) -> p b h w", w=W),
                    inner(abcA)[0:DIMS[0], k * IPC:(k + 1) * IPC],
                    pair(dw[0][0:DIMS[0]], k).rearrange("p h (b w) -> p b h w", w=W), ALU.mult).then_inc(h0_done, 1)
            matrices(16)
            dve.wait_ge(dw_in[1], 16 * NGR[1])
            for k in range(NCH):
                dve.wait_ge(pw0_ps, k + 1)
                nc.vector.scalar_tensor_tensor(
                    pair(h1, k), bank[k][0:DIMS[1], :].rearrange("p (h n) -> p h n", h=H),
                    ecol("pw0_b", DIMS[1]), pair(dw[1][0:DIMS[1]], k), ALU.add, ALU.mult).then_inc(h1_done, 1)
            matrices(16)
            dve.wait_ge(dw_in[2], 16 * NGR[2])
            for k in range(NCH):
                dve.wait_ge(pw1_ps, k + 1)
                nc.vector.scalar_tensor_tensor(
                    pair(h2, k), bank[k][:, :].rearrange("p (h n) -> p h n", h=H),
                    ecol("pw1_b"), pair(dw[2], k), ALU.add, ALU.mult).then_inc(h2_done, 1)
            dve.wait_ge(xb_done, 1)
            for k in range(NCH):
                im = slice(k * IPC, (k + 1) * IPC)
                dve.wait_ge(out_ps, k + 1)
                nc.vector.tensor_tensor(y_sb[:, im], bank[4 + k][:, :].rearrange("p (h b w) -> p b h w", h=H, b=IPC),
                                        x1[:, im], ALU.add).then_inc(y_done, 1)

        @block.tensor
        def _(pe):
            mm = nc.tensor.matmul
            pe.wait_ge(early_in, 16)
            pe.wait_ge(stats_done, B)
            gavg = ecol("gavg")
            mm(psM[:, 0:B], gavg, st[:, :, 1], start=True, stop=False)
            mm(psM[:, 0:B], gavg, st[:, :, 4], start=False, stop=True).then_inc(mean_ps, 1)
            pe.wait_ge(vpart_done, 1)
            mm(psV[:, 0:B], gavg, vpart[:, :, 0], start=True, stop=False)
            mm(psV[:, 0:B], gavg, vpart[:, :, 1], start=False, stop=True).then_inc(var_ps, 1)
            pe.wait_ge(normed_done, 1)
            mm(psQ[:, 0:C], ecol("wq"), normed[:, 0, :, :], start=True, stop=True).then_inc(qk_ps, 1)
            mm(psK[:, 0:C], ecol("wk"), normed[:, 0, :, :], start=True, stop=True).then_inc(qk_ps, 1)
            pe.wait_ge(normed_done, 2)
            mm(psVt[:, 0:C], normed[:, 1, :, :], ecol("wv"), start=True, stop=True).then_inc(v_ps, 1)
            pe.wait_ge(q_done, 1)
            pe.wait_ge(k_done, 1)
            mm(psS[:, 0:C], q_sb[:, :], k_sb[:, :], start=True, stop=True).then_inc(score_ps, 1)
            pe.wait_ge(pnorm_done, 1)
            nc.tensor.transpose(psP[:, 0:C], pnorm[:, :], ecol("ident")).then_inc(pT_ps, 1)
            pe.wait_ge(pT_done, 1)
            pe.wait_ge(v_done, 1)
            mm(psO[:, 0:C], v_sb[:, :], pT[:, :], start=True, stop=True).then_inc(o_ps, 1)
            pe.wait_ge(ysum_done, 1)
            mm(psM[:, 0:B], gavg, ysum[:, :], start=True, stop=True).then_inc(mean2_ps, 1)
            pe.wait_ge(v2_done, 1)
            mm(psV[:, 0:B], gavg, v2[:, :], start=True, stop=True).then_inc(var2_ps, 1)
            pe.wait_ge(late_in, 16)
            for k in range(NCH):
                pe.wait_ge(x1n_dve, x1n_need[k][0])
                if x1n_need[k][1]:
                    pe.wait_ge(x1n_act, x1n_need[k][1])
                mm(bank[k][:, :], lcol("w_in")[:, 0:C], x1n[:, k * IPC:(k + 1) * IPC, :], start=True, stop=True
                   ).then_inc(inA_ps, 1)
            for k in range(NCH):
                mm(bank[(4 + k) % 8][:, :], lcol("w_in")[:, C:2 * C], x1n[:, k * IPC:(k + 1) * IPC, :],
                   start=True, stop=True).then_inc(inB_ps, 1)
            pe.wait_ge(inB_done, NCH)
            for g in range(NG):
                pe.wait_ge(cin_in[g], 16)
                if g % QUAD == 0:
                    pe.wait_ge(toep_done, g // QUAD + 1)
                if g >= 3:
                    pe.wait_ge(conv_done, g - 2)
                for kx in range(K):
                    rows = cin[:, g, 0:ROW - ROW % PITCH].rearrange("p (b s) -> p b s", s=PITCH)
                    src = bass.AP(rows.tensor, rows.offset + kx, [rows.ap[0], [PITCH, B], [1, W]])
                    last = mm(conv_bank[g % 3][:, 0:BW], toep[:, g % (TQ * QUAD), kx, :, :], src,
                              start=(kx == 0), stop=(kx == K - 1))
                last.then_inc(conv_ps, 1)
                if g == 8:
                    for k in range(NCH):
                        pe.wait_ge(h0_done, k + 1)
                        mm(bank[k][0:DIMS[1], :], lcol("pw0", DIMS[0]), pair(h0, k), start=True, stop=True
                           ).then_inc(pw0_ps, 1)
                if g == 17:
                    for k in range(NCH):
                        pe.wait_ge(h1_done, k + 1)
                        mm(bank[k][:, :], lcol("pw1", DIMS[1]), pair(h1, k), start=True, stop=True
                           ).then_inc(pw1_ps, 1)
            pe.wait_ge(conv_done, NG)
            for k in range(NCH):
                pe.wait_ge(h2_done, k + 1)
                mm(bank[4 + k][:, :], lcol("w_out"), pair(h2, k), start=True, stop=True).then_inc(out_ps, 1)


def kernel(**inputs):
    import numpy as np
    import concourse.bacc as bacc
    from concourse.bass_utils import run_bass_kernel_spmd

    a = {k: np.ascontiguousarray(v) for k, v in inputs.items()}
    L0 = {k[8:]: v for k, v in a.items() if k.startswith("L0_conv_")}
    L1 = {k[8:]: v for k, v in a.items() if k.startswith("L1_conv_")}

    p = np.arange(C)
    same_group = (p[:, None] // GN == p[None, :] // GN)
    same_image = (p[:, None] // H == p[None, :] // H)
    early = np.zeros((C, E_N), np.float32)
    late = np.zeros((C, L_N), np.float32)

    def put(pack, cols, name, block):
        lo, hi = cols[name]
        pack[:block.shape[0], lo:lo + block.shape[1]] = block

    put(early, E_COL, "gavg", np.where(same_group, np.float32(1 / 8), np.float32(0)))
    put(early, E_COL, "ident", np.eye(C, dtype=np.float32))
    put(early, E_COL, "offmask", np.where(same_image, np.float32(0), np.float32(OFF_BLOCK)))
    put(early, E_COL, "blk", (p[:, None] // H == np.arange(GC)[None, :]).astype(np.float32))
    for name, w in (("wq", L0["Wq"]), ("wk", L0["Wk"]), ("wv", L0["Wv"])):
        put(early, E_COL, name, w.T)
    for name, v in (("bq", L0["bq"]), ("bk", L0["bk"]), ("bv", L0["bv"]), ("b_inA", L1["b_in"][:C]),
                    ("b_inB", L1["b_in"][C:]), ("pw0_b", L1["pw0_b"]), ("pw1_b", L1["pw1_b"]),
                    ("b_out", L1["b_out"])):
        put(early, E_COL, name, v[:, None])
    for name, w in (("w_in", L1["w_in"]), ("pw0", L1["pw0_w"]), ("pw1", L1["pw1_w"]), ("w_out", L1["w_out"])):
        put(late, L_COL, name, w.T)
    lo = E_COL["dw_b"][0]
    for s in range(3):
        first = sum(DIMS[:s])
        per = L1["dw_b"][first:first + DIMS[s]].reshape(GC, NGR[s])
        early[:, lo + G0[s]:lo + G0[s] + NGR[s]] = np.repeat(per, H, axis=0)
    taps = np.zeros((GC, H, NG, K, H), np.float32)
    for s in range(3):
        first = sum(DIMS[:s])
        w = L1["dw_w"][first:first + DIMS[s], 0].reshape(GC, NGR[s], K, K)
        for row_out in range(H):
            for row_in in range(max(0, row_out - PAD), min(H, row_out + PAD + 1)):
                taps[:, row_in, G0[s]:G0[s] + NGR[s], :, row_out] = w[:, :, row_in - row_out + PAD, :]
    taps = taps.reshape(C, NG, K, H)

    arrays = {"x": a["x"], "early": early, "late": late, "taps": taps}
    nc = bacc.Bacc("TRN2", target_bir_lowering=False, num_devices=1)
    args = [nc.dram_tensor(f"in_{n}", v.shape, F32, kind="ExternalInput").ap() for n, v in arrays.items()]
    out = nc.dram_tensor("out_0", (B, C, H, W), F32, kind="ExternalOutput").ap()
    build(nc, *args, out)
    r = run_bass_kernel_spmd(nc, [{f"in_{n}": v for n, v in arrays.items()}], core_ids=[0])
    return r.results[0]["out_0"]
```

```python
from contextlib import ExitStack

import concourse.bass as bass
from concourse import mybir

F32 = mybir.dt.float32
ALU = mybir.AluOpType
ACT = mybir.ActivationFunctionType
AX_X = mybir.AxisListType.X

C = 128
B, H, W = 8, 16, 16
HW = H * W
NTOK = B * HW
S = 4
GN = 4
K = 7
PAD = K // 2
GC = C // H
PITCH = W + PAD
ROW = 160
BW = B * W
CH = 512
NCH = NTOK // CH
IPC = CH // HW
QUAD = 4
TQ = 3
EPS = 1e-5
POOL_CHUNKS = (0, 1)
WARM = 16
OFF_BLOCK = -1e30

DIMS = (C // 4, C // 2, C)
NGR = [d // GC for d in DIMS]
G0 = [0, NGR[0], NGR[0] + NGR[1]]
NG = sum(NGR)
NQ = NG // QUAD
LAST = range(NG - 6, NG)

EARLY = [("wq", C), ("wk", C), ("wv", C), ("ident", C), ("offmask", C), ("blk", GC),
         ("bq", 1), ("bk", 1), ("bv", 1), ("b_inA", 1), ("b_inB", 1), ("pw0_b", 1), ("pw1_b", 1),
         ("b_out", 1), ("eps", 1), ("dw_b", NG)]
LATE = [("w_in", 2 * C), ("pw0", DIMS[1]), ("pw1", C), ("w_out", C)]


def columns(layout):
    at, out = 0, {}
    for name, n in layout:
        out[name] = (at, at + n)
        at += n
    return out, at


E_COL, E_N = columns(EARLY)
L_COL, L_N = columns(LATE)


def build(nc, x, gavg, early, late, taps, out):
    with ExitStack() as ctx:
        def sb(name, shape):
            return ctx.enter_context(nc.sbuf_tensor(name, shape, F32))

        def sem(name):
            return ctx.enter_context(nc.semaphore(name))

        x_sb = sb("x_sb", [C, B, H, W])
        x1 = sb("x1", [C, B, H, W])
        x1n = sb("x1n", [C, B, HW])
        g_sb = sb("g_sb", [C, C])
        e_sb = sb("e_sb", [C, E_N])
        l_sb = sb("l_sb", [C, L_N])
        taps_sb = sb("taps_sb", [C, NG, K, H])
        toep = sb("toep", [C, TQ * QUAD, K, GC, H])
        abcA = sb("abcA", [C, H, ROW])
        abcB = sb("abcB", [C, H, ROW])
        cin = sb("cin", [C, NG, ROW])
        cout = sb("cout", [C, NG, BW])
        dw = [sb(f"dw{i}", [C, H, BW]) for i in range(3)]
        h0 = sb("h0", [DIMS[0], H, BW])
        h1 = sb("h1", [DIMS[1], H, BW])
        h2 = x1n[:, :, :].rearrange("p b n -> p (b n)").rearrange("p (h n) -> p h n", h=H)
        y_sb = sb("y_sb", [C, B, H, W])

        st = sb("st", [C, B, 6])
        colsum = sb("colsum", [C, B, H, S])
        sums = sb("sums", [C, 2, B, H])
        pairs = sb("pairs", [C, len(POOL_CHUNKS) * IPC, HW // 2])
        dev = sb("dev", [C, B, 2])
        dev2 = sb("dev2", [C, B, 2])
        vpart = sb("vpart", [C, B, 2])
        std = sb("std", [C, B])
        warm = sb("warm", [C, 3])
        a1 = sb("a1", [C, B])
        b1 = sb("b1", [C, B])
        scaled = sb("scaled", [C, 2, B, H])
        normed = sb("normed", [C, 2, B, H])
        q_sb = sb("q_sb", [C, C])
        k_sb = sb("k_sb", [C, C])
        v_sb = sb("v_sb", [C, C])
        score = sb("score", [C, C])
        nmax = sb("nmax", [C, 1])
        probs = sb("probs", [C, C])
        rsum = sb("rsum", [C, 1])
        rinv = sb("rinv", [C, 1])
        pnorm = sb("pnorm", [C, C])
        pT = sb("pT", [C, C])
        o_sb = sb("o_sb", [C, B, H])
        mdiff = sb("mdiff", [C, B])
        msum = sb("msum", [C, B])
        m2 = sb("m2", [C, B])
        rcen = sb("rcen", [C, B, H])
        rsq = sb("rsq", [C, B])
        within = sb("within", [C, B])
        yrow = sb("yrow", [C, B, H])
        ysum = sb("ysum", [C, B])
        yd = sb("yd", [C, B, H])
        yd2 = sb("yd2", [C, B, H])
        yq = sb("yq", [C, B])
        v2 = sb("v2", [C, B])
        std2 = sb("std2", [C, B])
        a2 = sb("a2", [C, B])
        b2 = sb("b2", [C, B])

        bank = [ctx.enter_context(nc.psum_tensor(f"bank{i}", [C, CH], F32)) for i in range(8)]
        conv_bank = [bank[4], bank[5], bank[6]]
        psM, psV = bank[6], bank[7]
        psQ, psK, psVt, psS = bank[0], bank[1], bank[2], bank[3]
        psP, psO = bank[4], bank[5]

        def ecol(name, rows=C):
            a, b = E_COL[name]
            return e_sb[0:rows, a:b]

        def lcol(name, rows=C):
            a, b = L_COL[name]
            return l_sb[0:rows, a:b]

        x_in = [sem(f"x_in{i}") for i in range(NCH)]
        gavg_in, early_in, late_in = sem("gavg_in"), sem("early_in"), sem("late_in")
        taps_in = [sem(f"taps_in{i}") for i in range(3)]
        pairs_done, colsum_pool = sem("pairs_done"), sem("colsum_pool")
        stats_done, mean_ps, vpart_done, var_ps = sem("stats_done"), sem("mean_ps"), sem("vpart_done"), sem("var_ps")
        std_done, std2_done = sem("std_done"), sem("std2_done")
        normed_done, qk_ps, v_ps, q_done, k_done, v_done = (
            sem("normed_done"), sem("qk_ps"), sem("v_ps"), sem("q_done"), sem("k_done"), sem("v_done"))
        score_ps, score_done, exp_done, pnorm_done = sem("score_ps"), sem("score_done"), sem("exp_done"), sem("pnorm_done")
        pT_ps, pT_done, o_ps = sem("pT_ps"), sem("pT_done"), sem("o_ps")
        ysum_done, mean2_ps, v2_done, var2_ps = sem("ysum_done"), sem("mean2_ps"), sem("v2_done"), sem("var2_ps")
        affine_done = sem("affine_done")
        x1n_dve, x1n_act = sem("x1n_dve"), sem("x1n_act")
        inA_ps, inB_ps, inA_done, inB_done = sem("inA_ps"), sem("inB_ps"), sem("inA_done"), sem("inB_done")
        toep_done = sem("toep_done")
        cin_in = [sem(f"cin_in{g}") for g in range(NG)]
        conv_ps, conv_done = sem("conv_ps"), sem("conv_done")
        dw_in = [sem(f"dw_in{i}") for i in range(3)]
        dw_last = sem("dw_last")
        h0_done, pw0_ps, h1_done, pw1_ps, h2_done, out_ps, y_done = (
            sem("h0_done"), sem("pw0_ps"), sem("h1_done"), sem("pw1_ps"), sem("h2_done"), sem("out_ps"),
            sem("y_done"))
        stored = sem("stored")
        dve_step = sem("dve_step")
        pads_done = sem("pads_done")

        ACT_IMAGES = (3, 5, 7)
        x1n_need = []
        for k in range(NCH):
            upto = range((k + 1) * IPC)
            x1n_need.append((len([b for b in upto if b not in ACT_IMAGES]), len([b for b in upto if b in ACT_IMAGES])))

        def inner(t):
            return t[:, :, PAD:PAD + B * PITCH].rearrange("p h (b s) -> p b h s", s=PITCH)[:, :, :, 0:W]

        def pair(t, k):
            return t[:, :, k * IPC * W:(k + 1) * IPC * W]

        block = ctx.enter_context(nc.Block())

        @block.sync
        def _(sp):
            for k in range(NCH):
                sp.dma_start(x_sb[:, k * IPC:(k + 1) * IPC, :, :].rearrange("c b h w -> c b (h w)"),
                             x[k * IPC:(k + 1) * IPC].rearrange("b c h w -> c b (h w)")).then_inc(x_in[k], 16)
            sp.dma_start(e_sb[:, :], early).then_inc(early_in, 16)
            for s in range(3):
                sp.dma_start(taps_sb[:, G0[s]:G0[s] + NGR[s]], taps[:, G0[s]:G0[s] + NGR[s]]).then_inc(taps_in[s], 16)
            sp.dma_start(l_sb[:, :], late).then_inc(late_in, 16)
            sp.wait_ge(pads_done, 1)
            for s, (tile, base, ready) in enumerate(((abcA, DIMS[0], inA_done), (abcA, 2 * DIMS[0], inA_done),
                                                     (abcB, 0, inB_done))):
                sp.wait_ge(ready, NCH)
                for j in range(NGR[s]):
                    g = G0[s] + j
                    sp.dma_start(cin[:, g, :], tile[base + j:base + j + NGR[s] * (GC - 1) + 1:NGR[s], :, :]
                                 ).then_inc(cin_in[g], 16)
            for s in range(3):
                for j in range(NGR[s]):
                    g = G0[s] + j
                    if g not in LAST:
                        continue
                    sp.wait_ge(conv_done, g + 1)
                    sp.dma_start(dw[s][j:j + NGR[s] * (GC - 1) + 1:NGR[s], :, :], cout[:, g, :]
                                 ).then_inc(dw_last, 16)
            for k in range(NCH):
                sp.wait_ge(y_done, k + 1)
                sp.dma_start(out[k * IPC:(k + 1) * IPC].rearrange("b c h w -> c b (h w)"),
                             y_sb[:, k * IPC:(k + 1) * IPC, :, :].rearrange("c b h w -> c b (h w)")
                             ).then_inc(stored, 16)
            sp.wait_ge(stored, 16 * NCH)

        @block.gpsimd
        def _(pool):
            for k in POOL_CHUNKS:
                im = slice(k * IPC, (k + 1) * IPC)
                pool.wait_ge(x_in[k], 16)
                xs = x_sb[:, im].rearrange("p b h w -> p (b h w)").rearrange("p (n s) -> p n s", s=2)
                nc.gpsimd.tensor_tensor(pairs[:, im], xs[:, :, 0], xs[:, :, 1], ALU.add).then_inc(pairs_done, 1)
                pool.wait_ge(pairs_done, k + 1)
                ps = pairs[:, im].rearrange("p b n -> p (b n)").rearrange("p (n s) -> p n s", s=2)
                nc.gpsimd.tensor_tensor(colsum[:, im].rearrange("p b h v -> p (b h v)"), ps[:, :, 0], ps[:, :, 1],
                                        ALU.add).then_inc(colsum_pool, 1)
            nc.gpsimd.memset(abcA[:, :, :], 0.0)
            nc.gpsimd.memset(abcB[:, :, :], 0.0).then_inc(pads_done, 1)
            pool.wait_ge(early_in, 16)
            for s in range(3):
                for j in range(NGR[s]):
                    g = G0[s] + j
                    if g in LAST:
                        continue
                    pool.wait_ge(conv_done, g + 1)
                    pool.dma_start(dw[s][j:j + NGR[s] * (GC - 1) + 1:NGR[s], :, :], cout[:, g, :]
                                   ).then_inc(dw_in[s], 16)

        @block.scalar
        def _(act):
            act.dma_start(g_sb[:, :], gavg).then_inc(gavg_in, 16)
            act.wait_ge(gavg_in, 16)
            nc.scalar.activation(warm[:, 0:1], g_sb[:, 0:1], ACT.Sqrt)
            act.wait_ge(early_in, 16)
            act.wait_ge(var_ps, 1)
            nc.scalar.activation(std[:, :], psV[:, 0:B], ACT.Sqrt, bias=ecol("eps")).then_inc(std_done, 1)
            nc.scalar.activation(warm[:, 1:2], g_sb[:, 0:1], ACT.Exp)
            act.wait_ge(qk_ps, 1)
            nc.scalar.activation(q_sb[:, :], psQ[:, 0:C], ACT.Identity, bias=ecol("bq")).then_inc(q_done, 1)
            act.wait_ge(v_ps, 1)
            nc.scalar.copy(v_sb[:, :], psVt[:, 0:C]).then_inc(v_done, 1)
            act.wait_ge(score_done, 1)
            nc.scalar.activation(probs[:, :], score[:, :], ACT.Exp, bias=nmax[:, :], accum_out=rsum[:, :]
                                 ).then_inc(exp_done, 1)
            nc.scalar.activation(warm[:, 2:3], g_sb[:, 0:1], ACT.Sqrt)
            act.wait_ge(var2_ps, 1)
            nc.scalar.activation(std2[:, :], psV[:, 0:B], ACT.Sqrt, bias=ecol("eps"), scale=8.0 / (GN * HW)
                                 ).then_inc(std2_done, 1)
            act.wait_ge(affine_done, 1)
            for b in ACT_IMAGES:
                nc.scalar.activation(x1n[:, b, :], x1[:, b, :, :].rearrange("p h w -> p (h w)"), ACT.Identity,
                                     bias=b2[:, b:b + 1], scale=a2[:, b:b + 1]).then_inc(x1n_act, 1)
            act.wait_ge(pads_done, 1)
            for k in range(NCH):
                act.wait_ge(inA_ps, k + 1)
                nc.scalar.activation(inner(abcA)[:, k * IPC:(k + 1) * IPC],
                                     bank[k][:, :].rearrange("p (b h w) -> p b h w", b=IPC, h=H),
                                     ACT.Identity, bias=ecol("b_inA")).then_inc(inA_done, 1)
            for g in range(NG):
                act.wait_ge(conv_ps, g + 1)
                nc.scalar.activation(cout[:, g, :], conv_bank[g % 3][:, 0:BW], ACT.Identity,
                                     bias=ecol("dw_b")[:, g:g + 1]).then_inc(conv_done, 1)
            for k in range(NCH):
                act.wait_ge(out_ps, k + 1)
                nc.scalar.activation(y_sb[:, k * IPC:(k + 1) * IPC],
                                     bank[4 + k][:, :].rearrange("p (h b w) -> p b h w", h=H, b=IPC),
                                     ACT.Identity, bias=ecol("b_out")).then_inc(y_done, 1)

        @block.vector
        def _(dve):
            steps = [0]

            def link(ins):
                steps[0] += 1
                ins.then_inc(dve_step, 1)
                dve.wait_ge(dve_step, steps[0])

            todo = [(q, c) for q in range(NQ) for c in range(GC)]

            def matrices(n):
                for _ in range(n):
                    q, c = todo.pop(0)
                    if c == 0:
                        s = max(i for i in range(3) if G0[i] <= q * QUAD)
                        if q * QUAD == G0[s]:
                            dve.wait_ge(taps_in[s], 16)
                        if q >= TQ:
                            dve.wait_ge(conv_ps, (q - TQ + 1) * QUAD)
                    at = q % TQ * QUAD
                    ins = nc.vector.tensor_scalar(
                        toep[:, at:at + QUAD, :, c, :],
                        taps_sb[:, q * QUAD:(q + 1) * QUAD, :, :],
                        ecol("blk")[:, c:c + 1], None, ALU.mult)
                    if c == GC - 1:
                        ins.then_inc(toep_done, 1)

            for k in range(NCH):
                dve.wait_ge(x_in[k], 16)
                for b in range(k * IPC, (k + 1) * IPC):
                    nc.vector.bn_stats(st[:, b, :], x_sb[:, b, :, :].rearrange("p h w -> p (h w)")
                                       ).then_inc(stats_done, 1)

            def column_sums(k):
                im = slice(k * IPC, (k + 1) * IPC)
                return nc.vector.tensor_reduce(
                    colsum[:, im], x_sb[:, im].rearrange("p b h (v s) -> p b h v s", s=S), AX_X, ALU.add)

            column_sums(2)
            dve.wait_ge(stats_done, B)
            dve.wait_ge(mean_ps, 1)
            link(nc.vector.tensor_tensor(dev[:, :, :], st[:, :, 1:6:3],
                                         psM[:, 0:B].unsqueeze(2).to_broadcast([C, B, 2]), ALU.subtract))
            link(nc.vector.tensor_tensor(dev2[:, :, :], dev[:, :, :], dev[:, :, :], ALU.mult))
            nc.vector.scalar_tensor_tensor(vpart[:, :, :], st[:, :, 2:6:3], 2.0 / HW, dev2[:, :, :],
                                           ALU.mult, ALU.add).then_inc(vpart_done, 1)
            link(column_sums(3))
            dve.wait_ge(colsum_pool, len(POOL_CHUNKS))
            link(nc.vector.tensor_reduce(
                sums[:, 0, :, :], colsum[:, :, :, :].rearrange("p b (u s) v -> p (b u) v s", s=S), AX_X, ALU.add))
            dve.wait_ge(std_done, 1)
            link(nc.vector.reciprocal(a1[:, :], std[:, :]))
            nc.vector.scalar_tensor_tensor(b1[:, :], psM[:, 0:B], -1.0, a1[:, :], ALU.mult, ALU.mult)

            def normalise(half):
                link(nc.vector.tensor_tensor(scaled[:, half, :, :], sums[:, half, :, :],
                                             a1[:, :].unsqueeze(2).to_broadcast([C, B, H]), ALU.mult))
                nc.vector.scalar_tensor_tensor(normed[:, half, :, :], scaled[:, half, :, :], 1.0 / H,
                                               b1[:, :].unsqueeze(2).to_broadcast([C, B, H]),
                                               ALU.mult, ALU.add).then_inc(normed_done, 1)

            normalise(0)
            link(nc.vector.tensor_reduce(sums[:, 1, :, :], colsum[:, :, :, :], AX_X, ALU.add))
            normalise(1)
            dve.wait_ge(early_in, 16)
            link(nc.vector.tensor_tensor(mdiff[:, :], st[:, :, 1], st[:, :, 4], ALU.subtract))
            nc.vector.tensor_tensor(msum[:, :], st[:, :, 1], st[:, :, 4], ALU.add)
            nc.vector.tensor_tensor(m2[:, :], st[:, :, 2], st[:, :, 5], ALU.add)
            dve.wait_ge(qk_ps, 2)
            nc.vector.tensor_scalar(k_sb[:, :], psK[:, 0:C], ecol("bk"), None, ALU.add).then_inc(k_done, 1)
            link(nc.vector.tensor_tensor(mdiff[:, :], mdiff[:, :], mdiff[:, :], ALU.mult))
            link(nc.vector.scalar_tensor_tensor(rcen[:, :, :], msum[:, :].unsqueeze(2).to_broadcast([C, B, H]),
                                                -W / 2.0, sums[:, 1, :, :], ALU.mult, ALU.add))
            dve.wait_ge(score_ps, 1)
            link(nc.vector.scalar_tensor_tensor(score[:, :], psS[:, 0:C], float(C) ** -0.5, ecol("offmask"),
                                                ALU.mult, ALU.add))
            nc.vector.tensor_reduce(nmax[:, :], score[:, :], AX_X, ALU.max, negate=True).then_inc(score_done, 1)
            link(nc.vector.scalar_tensor_tensor(m2[:, :], mdiff[:, :], HW / 4.0, m2[:, :], ALU.mult, ALU.add))
            link(nc.vector.tensor_tensor(rcen[:, :, :], rcen[:, :, :], rcen[:, :, :], ALU.mult))
            link(nc.vector.tensor_reduce(rsq[:, :], rcen[:, :, :], AX_X, ALU.add))
            link(nc.vector.scalar_tensor_tensor(within[:, :], rsq[:, :], -1.0 / W, m2[:, :], ALU.mult, ALU.add))
            nc.vector.tensor_scalar(within[:, :], within[:, :], 0.0, None, ALU.max)
            dve.wait_ge(exp_done, 1)
            link(nc.vector.reciprocal(rinv[:, :], rsum[:, :]))
            nc.vector.tensor_scalar(pnorm[:, :], probs[:, :], rinv[:, :], None, ALU.mult).then_inc(pnorm_done, 1)
            matrices(2)
            dve.wait_ge(pT_ps, 1)
            nc.vector.tensor_copy(pT[:, :], psP[:, 0:C]).then_inc(pT_done, 1)
            matrices(2)
            dve.wait_ge(o_ps, 1)
            link(nc.vector.tensor_scalar(o_sb[:, :, :].rearrange("p b h -> p (b h)"), psO[:, 0:C], ecol("bv"),
                                         float(W), ALU.add, ALU.mult))
            link(nc.vector.scalar_tensor_tensor(yrow[:, :, :], sums[:, 1, :, :], 1.0 / W, o_sb[:, :, :],
                                                ALU.mult, ALU.add))
            nc.vector.tensor_reduce(ysum[:, :], yrow[:, :, :], AX_X, ALU.add).then_inc(ysum_done, 1)

            def residual(k):
                im = slice(k * IPC, (k + 1) * IPC)
                return nc.vector.tensor_tensor(
                    x1[:, im].rearrange("p b h w -> p (b h) w"), x_sb[:, im].rearrange("p b h w -> p (b h) w"),
                    o_sb[:, im].rearrange("p b h -> p (b h)").unsqueeze(2).to_broadcast([C, IPC * H, W]), ALU.add)

            residual(0)
            dve.wait_ge(mean2_ps, 1)
            link(nc.vector.scalar_tensor_tensor(yd[:, :, :], psM[:, 0:B].unsqueeze(2).to_broadcast([C, B, H]),
                                                -8.0 / (GN * H), yrow[:, :, :], ALU.mult, ALU.add))
            link(nc.vector.tensor_tensor(yd2[:, :, :], yd[:, :, :], yd[:, :, :], ALU.mult))
            link(nc.vector.tensor_reduce(yq[:, :], yd2[:, :, :], AX_X, ALU.add))
            nc.vector.scalar_tensor_tensor(v2[:, :], yq[:, :], float(W), within[:, :], ALU.mult, ALU.add
                                           ).then_inc(v2_done, 1)
            residual(1)
            residual(2)
            link(residual(3))
            dve.wait_ge(std2_done, 1)
            link(nc.vector.reciprocal(a2[:, :], std2[:, :]))
            ins = nc.vector.scalar_tensor_tensor(b2[:, :], psM[:, 0:B], -8.0 / (GN * H), a2[:, :],
                                                 ALU.mult, ALU.mult)
            ins.then_inc(affine_done, 1)
            dve.wait_ge(affine_done, 1)
            for b in range(B):
                if b not in ACT_IMAGES:
                    nc.vector.tensor_scalar(x1n[:, b, :], x1[:, b, :, :].rearrange("p h w -> p (h w)"),
                                            a2[:, b:b + 1], b2[:, b:b + 1], ALU.mult, ALU.add
                                            ).then_inc(x1n_dve, 1)
            matrices(8)
            dve.wait_ge(pads_done, 1)
            for k in range(NCH):
                dve.wait_ge(inB_ps, k + 1)
                nc.vector.tensor_scalar(inner(abcB)[:, k * IPC:(k + 1) * IPC],
                                        bank[k if k < 0 else (4 + k) % 8][:, :].rearrange(
                                            "p (b h w) -> p b h w", b=IPC, h=H),
                                        ecol("b_inB"), None, ALU.add).then_inc(inB_done, 1)
            matrices(8)
            dve.wait_ge(inA_done, NCH)
            dve.wait_ge(dw_in[0], 16 * NGR[0])
            for k in range(NCH):
                nc.vector.tensor_tensor(
                    pair(h0, k).rearrange("p h (b w) -> p b h w", w=W),
                    inner(abcA)[0:DIMS[0], k * IPC:(k + 1) * IPC],
                    pair(dw[0][0:DIMS[0]], k).rearrange("p h (b w) -> p b h w", w=W), ALU.mult).then_inc(h0_done, 1)
            matrices(16)
            dve.wait_ge(dw_in[1], 16 * NGR[1])
            for k in range(NCH):
                dve.wait_ge(pw0_ps, k + 1)
                nc.vector.scalar_tensor_tensor(
                    pair(h1, k), bank[k][0:DIMS[1], :].rearrange("p (h n) -> p h n", h=H),
                    ecol("pw0_b", DIMS[1]), pair(dw[1][0:DIMS[1]], k), ALU.add, ALU.mult).then_inc(h1_done, 1)
            matrices(len(todo))
            dve.wait_ge(dw_in[2], 16 * (NGR[2] - len(LAST)))
            dve.wait_ge(dw_last, 16 * len(LAST))
            for k in range(NCH):
                dve.wait_ge(pw1_ps, k + 1)
                nc.vector.scalar_tensor_tensor(
                    pair(h2, k), bank[k][:, :].rearrange("p (h n) -> p h n", h=H),
                    ecol("pw1_b"), pair(dw[2], k), ALU.add, ALU.mult).then_inc(h2_done, 1)

        @block.tensor
        def _(pe):
            mm = nc.tensor.matmul
            gavg = g_sb[:, :]
            pe.wait_ge(gavg_in, 16)
            pe.wait_ge(stats_done, B)
            mm(psM[:, 0:B], gavg, st[:, :, 1], start=True, stop=False)
            mm(psM[:, 0:B], gavg, st[:, :, 4], start=False, stop=True).then_inc(mean_ps, 1)
            pe.wait_ge(vpart_done, 1)
            mm(psV[:, 0:B], gavg, vpart[:, :, 0], start=True, stop=False)
            mm(psV[:, 0:B], gavg, vpart[:, :, 1], start=False, stop=True).then_inc(var_ps, 1)
            pe.wait_ge(early_in, 16)
            pe.wait_ge(normed_done, 1)
            mm(psQ[:, 0:C], ecol("wq"), normed[:, 0, :, :], start=True, stop=True).then_inc(qk_ps, 1)
            mm(psK[:, 0:C], ecol("wk"), normed[:, 0, :, :], start=True, stop=True).then_inc(qk_ps, 1)
            pe.wait_ge(normed_done, 2)
            mm(psVt[:, 0:C], normed[:, 1, :, :], ecol("wv"), start=True, stop=True).then_inc(v_ps, 1)
            pe.wait_ge(q_done, 1)
            pe.wait_ge(k_done, 1)
            mm(psS[:, 0:C], q_sb[:, :], k_sb[:, :], start=True, stop=True).then_inc(score_ps, 1)
            pe.wait_ge(pnorm_done, 1)
            nc.tensor.transpose(psP[:, 0:C], pnorm[:, :], ecol("ident")).then_inc(pT_ps, 1)
            pe.wait_ge(pT_done, 1)
            pe.wait_ge(v_done, 1)
            mm(psO[:, 0:C], v_sb[:, :], pT[:, :], start=True, stop=True).then_inc(o_ps, 1)
            pe.wait_ge(ysum_done, 1)
            mm(psM[:, 0:B], gavg, ysum[:, :], start=True, stop=True).then_inc(mean2_ps, 1)
            pe.wait_ge(v2_done, 1)
            mm(psV[:, 0:B], gavg, v2[:, :], start=True, stop=True).then_inc(var2_ps, 1)
            for _ in range(WARM):
                mm(bank[5][:, 0:C], ecol("ident"), ecol("ident"), start=True, stop=True)
            pe.wait_ge(late_in, 16)
            for k in range(NCH):
                pe.wait_ge(x1n_dve, x1n_need[k][0])
                if x1n_need[k][1]:
                    pe.wait_ge(x1n_act, x1n_need[k][1])
                mm(bank[k][:, :], lcol("w_in")[:, 0:C], x1n[:, k * IPC:(k + 1) * IPC, :], start=True, stop=True
                   ).then_inc(inA_ps, 1)
            for k in range(NCH):
                mm(bank[(4 + k) % 8][:, :], lcol("w_in")[:, C:2 * C], x1n[:, k * IPC:(k + 1) * IPC, :],
                   start=True, stop=True).then_inc(inB_ps, 1)
            pe.wait_ge(inB_done, NCH)
            for g in range(NG):
                pe.wait_ge(cin_in[g], 16)
                if g % QUAD == 0:
                    pe.wait_ge(toep_done, g // QUAD + 1)
                if g >= 3:
                    pe.wait_ge(conv_done, g - 2)
                for kx in range(K):
                    rows = cin[:, g, 0:ROW - ROW % PITCH].rearrange("p (b s) -> p b s", s=PITCH)
                    src = bass.AP(rows.tensor, rows.offset + kx, [rows.ap[0], [PITCH, B], [1, W]])
                    last = mm(conv_bank[g % 3][:, 0:BW], toep[:, g % (TQ * QUAD), kx, :, :], src,
                              start=(kx == 0), stop=(kx == K - 1))
                last.then_inc(conv_ps, 1)
                if g == 8:
                    for k in range(NCH):
                        pe.wait_ge(h0_done, k + 1)
                        mm(bank[k][0:DIMS[1], :], lcol("pw0", DIMS[0]), pair(h0, k), start=True, stop=True
                           ).then_inc(pw0_ps, 1)
                if g == 17:
                    for k in range(NCH):
                        pe.wait_ge(h1_done, k + 1)
                        mm(bank[k][:, :], lcol("pw1", DIMS[1]), pair(h1, k), start=True, stop=True
                           ).then_inc(pw1_ps, 1)
            pe.wait_ge(conv_done, NG)
            for k in range(NCH):
                mm(bank[4 + k][:, :], ecol("ident"), x1[:, k * IPC:(k + 1) * IPC, :, :].rearrange(
                    "p b h w -> p h b w"), start=True, stop=False)
            for k in range(NCH):
                pe.wait_ge(h2_done, k + 1)
                mm(bank[4 + k][:, :], lcol("w_out"), pair(h2, k), start=False, stop=True).then_inc(out_ps, 1)


def kernel(**inputs):
    import numpy as np
    import concourse.bacc as bacc
    from concourse.bass_utils import run_bass_kernel_spmd

    a = {k: np.ascontiguousarray(v) for k, v in inputs.items()}
    L0 = {k[8:]: v for k, v in a.items() if k.startswith("L0_conv_")}
    L1 = {k[8:]: v for k, v in a.items() if k.startswith("L1_conv_")}

    p = np.arange(C)
    same_group = (p[:, None] // GN == p[None, :] // GN)
    same_image = (p[:, None] // H == p[None, :] // H)
    early = np.zeros((C, E_N), np.float32)
    late = np.zeros((C, L_N), np.float32)

    def put(pack, cols, name, block):
        lo, hi = cols[name]
        pack[:block.shape[0], lo:lo + block.shape[1]] = block

    gavg = np.where(same_group, np.float32(1 / 8), np.float32(0))
    put(early, E_COL, "eps", np.full((C, 1), EPS, np.float32))
    put(early, E_COL, "ident", np.eye(C, dtype=np.float32))
    put(early, E_COL, "offmask", np.where(same_image, np.float32(0), np.float32(OFF_BLOCK)))
    put(early, E_COL, "blk", (p[:, None] // H == np.arange(GC)[None, :]).astype(np.float32))
    for name, w in (("wq", L0["Wq"]), ("wk", L0["Wk"]), ("wv", L0["Wv"])):
        put(early, E_COL, name, w.T)
    for name, v in (("bq", L0["bq"]), ("bk", L0["bk"]), ("bv", L0["bv"]), ("b_inA", L1["b_in"][:C]),
                    ("b_inB", L1["b_in"][C:]), ("pw0_b", L1["pw0_b"]), ("pw1_b", L1["pw1_b"]),
                    ("b_out", L1["b_out"])):
        put(early, E_COL, name, v[:, None])
    for name, w in (("w_in", L1["w_in"]), ("pw0", L1["pw0_w"]), ("pw1", L1["pw1_w"]), ("w_out", L1["w_out"])):
        put(late, L_COL, name, w.T)
    lo = E_COL["dw_b"][0]
    for s in range(3):
        first = sum(DIMS[:s])
        per = L1["dw_b"][first:first + DIMS[s]].reshape(GC, NGR[s])
        early[:, lo + G0[s]:lo + G0[s] + NGR[s]] = np.repeat(per, H, axis=0)
    taps = np.zeros((GC, H, NG, K, H), np.float32)
    for s in range(3):
        first = sum(DIMS[:s])
        w = L1["dw_w"][first:first + DIMS[s], 0].reshape(GC, NGR[s], K, K)
        for row_out in range(H):
            for row_in in range(max(0, row_out - PAD), min(H, row_out + PAD + 1)):
                taps[:, row_in, G0[s]:G0[s] + NGR[s], :, row_out] = w[:, :, row_in - row_out + PAD, :]
    taps = taps.reshape(C, NG, K, H)

    arrays = {"x": a["x"], "gavg": gavg, "early": early, "late": late, "taps": taps}
    nc = bacc.Bacc("TRN2", target_bir_lowering=False, num_devices=1)
    args = [nc.dram_tensor(f"in_{n}", v.shape, F32, kind="ExternalInput").ap() for n, v in arrays.items()]
    out = nc.dram_tensor("out_0", (B, C, H, W), F32, kind="ExternalOutput").ap()
    build(nc, *args, out)
    r = run_bass_kernel_spmd(nc, [{f"in_{n}": v for n, v in arrays.items()}], core_ids=[0])
    return r.results[0]["out_0"]
```

```python
from contextlib import ExitStack

import concourse.bass as bass
from concourse import mybir

F32 = mybir.dt.float32
F32R = mybir.dt.float32r
ALU = mybir.AluOpType
ACT = mybir.ActivationFunctionType
AX_X = mybir.AxisListType.X

C = 128
B, H, W = 8, 16, 16
HW = H * W
NTOK = B * HW
S = 4
GN = 4
K = 7
PAD = K // 2
GC = C // H
PITCH = W + PAD
ROW = 160
BW = B * W
CH = 512
NCH = NTOK // CH
IPC = CH // HW
QUAD = 4
EPS = 1e-5
POOL_CHUNKS = (0, 1, 3)
POOL_RESIDUAL_AT = 3
POOL_RESIDUAL = (1, 2, 3)
ACT_IMAGES = (3, 5, 7)
WARM = (6, 2, 6, 5, 2, 3, 3, 5)
DVE_BLOCKS = [(0, c) for c in range(5, GC)] + [(3, c) for c in range(6)]
POOL_BLOCKS = [(q, c) for q in (1, 2) for c in range(GC)]
ACT_BLOCKS = [(0, c) for c in range(5)] + [(3, c) for c in range(6, GC)] + [(q, c) for q in (4, 5) for c in range(GC)]
ACT_HEAD = 5
COUT = 16
H0_TWICE_AT = 9
H0_HI_AT, PW0_AFTER, P0_AT, H1_HI_AT = 6, 14, 15, 17
ROWS = IPC * H + (IPC - 1) * PAD
STACK = PAD + (ROWS + 2 * PAD) * PITCH
OFF_BLOCK = -1e30

DIMS = (C // 4, C // 2, C)
DVE_CH = 32
DVE_AT = DIMS[2] - DVE_CH
MOVED_BY_DVE = (0, 1)
ACCS = 2
PARTS = ((0, 0, 4, 0, 32), (1, 0, 4, 0, 64), (1, 32, 4, 1, 0), (2, 0, DVE_AT // GC, 1, 32))
GROUPS = [(part, j) for part in PARTS for j in range(part[2])]
G0 = [[part[0] for part, _ in GROUPS].index(s) for s in range(3)]
NGR = [[part[0] for part, _ in GROUPS].count(s) for s in range(3)]
NG = sum(NGR)
NQ = NG // QUAD

EARLY = [("wq", C), ("wk", C), ("wv", C), ("ident", C), ("offmask", C), ("blk", GC),
         ("bq", 1), ("bk", 1), ("bv", 1), ("b_inA", 1), ("b_inB", 1), ("pw0_b", 1), ("pw1_b", 1),
         ("b_out", 1), ("eps", 1), ("dw_b", NG)]
LATE = [("dve_taps", K * K), ("dve_bias", 1), ("w_in", 2 * C), ("pw0", DIMS[1]), ("pw1", C), ("w_out", C)]


def columns(layout):
    at, out = 0, {}
    for name, n in layout:
        out[name] = (at, at + n)
        at += n
    return out, at


E_COL, E_N = columns(EARLY)
L_COL, L_N = columns(LATE)


def build(nc, x, gavg, early, late, taps, out):
    with ExitStack() as ctx:
        def sb(name, shape, dt=F32):
            return ctx.enter_context(nc.sbuf_tensor(name, shape, dt))

        def sem(name):
            return ctx.enter_context(nc.semaphore(name))

        x_sb = sb("x_sb", [C, B, H, W])
        x1 = sb("x1", [C, B, H, W])
        x1n = sb("x1n", [C, B, HW])
        g_sb = sb("g_sb", [C, C])
        e_sb = sb("e_sb", [C, E_N])
        l_sb = sb("l_sb", [C, L_N])
        taps_sb = sb("taps_sb", [C, NG, K, H])
        toep = sb("toep", [C, NG, K, GC, H])
        abcA = sb("abcA", [C, H, ROW])
        abcB = sb("abcB", [C, H, ROW])
        cin = sb("cin", [C, NG, ROW])
        cout = x1n[:, :, :].rearrange("p b n -> p (b n)").rearrange("p (g n) -> p g n", n=BW)
        dw = [sb("dw0", [C, H, BW]),
              x_sb[:, :, :, :].rearrange("p b h w -> p (b h w)").rearrange("p (h n) -> p h n", h=H),
              sb("dw2", [C, H, BW])]
        abcU = sb("abcU", [C, NCH, STACK])
        stack = sb("stack", [C, STACK])
        acc = sb("acc", [C, ACCS, ROWS, W])
        summed = sb("summed", [C, IPC, HW])
        p0 = abcA[:, :, :].rearrange("p h r -> p (h r)")[0:DIMS[1], 0:NTOK].rearrange("p (k h n) -> p k h n", k=NCH, h=H)
        dwU = abcU[:, :, :].rearrange("p k n -> p (k n)")[:, 0:NTOK].rearrange(
            "p (b h w) -> p b h w", b=B, h=H)
        parts = sb("parts", [C, H, BW], F32R)
        parts0 = parts[:, :, :].rearrange("p h n -> p (h n)").rearrange("p (k n) -> p k n", k=NCH)
        pw0_parts = sb("pw0_parts", [C, DIMS[1]], F32R)
        pw1_hi, pw1_lo = (sb(n, [2 * DIMS[1], C], F32R) for n in ("pw1_hi", "pw1_lo"))

        room = [[t[:, :, :].rearrange("p h n -> p (h n)"), 0] for t in (dw[0], dw[2])]

        def tmp(*shape):
            n = 1
            for d in shape:
                n *= d
            r = next(r for r in room if r[1] + n <= NTOK)
            at, r[1] = r[1], r[1] + n
            names = "abc"[:len(shape)]
            dims = {m: d for m, d in zip(names, shape)}
            return r[0][:, at:at + n].rearrange(f"p ({' '.join(names)}) -> p {' '.join(names)}", **dims)

        st = sb("st", [C, B, 6])
        colsum = tmp(B, H, S)
        sums = tmp(2, B, H)
        pairs = tmp(len(POOL_CHUNKS) * IPC, HW // 2)
        dev = sb("dev", [C, B, 2])
        dev2 = sb("dev2", [C, B, 2])
        vpart = sb("vpart", [C, B, 2])
        std = sb("std", [C, B])
        warm = sb("warm", [C, 3])
        a1 = sb("a1", [C, B])
        centred = tmp(2, B, H)
        normed = tmp(2, B, H)
        q_sb = tmp(C)
        k_sb = tmp(C)
        v_sb = tmp(C)
        score = tmp(C)
        nmax = sb("nmax", [C, 1])
        probs = tmp(C)
        rsum = sb("rsum", [C, 1])
        rinv = sb("rinv", [C, 1])
        pnorm = tmp(C)
        pT = tmp(C)
        o_sb = tmp(B, H)
        mdiff = sb("mdiff", [C, B])
        msum = sb("msum", [C, B])
        m2 = sb("m2", [C, B])
        rcen = tmp(B, H)
        rsq = sb("rsq", [C, B])
        within = sb("within", [C, B])
        vbias = sb("vbias", [C, 1])
        xrow = tmp(B, H)
        yrow = tmp(B, H)
        ysum = sb("ysum", [C, B])
        yd = tmp(B, H)
        yd2 = tmp(B, H)
        yq = sb("yq", [C, B])
        v2 = sb("v2", [C, B])
        std2 = sb("std2", [C, B])
        mean2 = sb("mean2", [C, B])
        a2 = sb("a2", [C, B])
        b2 = sb("b2", [C, B])

        bank = [ctx.enter_context(nc.psum_tensor(f"bank{i}", [C, CH], F32)) for i in range(8)]
        conv_bank = [bank[4], bank[5], bank[6]]
        psM, psV = bank[6], bank[7]
        psQ, psK, psVt, psS = bank[0], bank[1], bank[2], bank[3]
        psP, psO = bank[4], bank[0]
        unread = bank[5]

        def ecol(name, rows=C):
            a, b = E_COL[name]
            return e_sb[0:rows, a:b]

        def lcol(name, rows=C):
            a, b = L_COL[name]
            return l_sb[0:rows, a:b]

        x_in = [sem(f"x_in{i}") for i in range(NCH)]
        gavg_in, early_in, late_in = sem("gavg_in"), sem("early_in"), sem("late_in")
        taps_in = [sem(f"taps_in{i}") for i in range(3)]
        pairs_done, colsum_pool = sem("pairs_done"), sem("colsum_pool")
        stats_done, mean_ps, vpart_done, var_ps = sem("stats_done"), sem("mean_ps"), sem("vpart_done"), sem("var_ps")
        std_done, std2_done = sem("std_done"), sem("std2_done")
        normed_done, qk_ps, v_ps, q_done, k_done, v_done = (
            sem("normed_done"), sem("qk_ps"), sem("v_ps"), sem("q_done"), sem("k_done"), sem("v_done"))
        score_ps, score_done, exp_done, pnorm_done = sem("score_ps"), sem("score_done"), sem("exp_done"), sem("pnorm_done")
        pT_ps, pT_done, o_ps = sem("pT_ps"), sem("pT_done"), sem("o_ps")
        ysum_done, mean2_ps, v2_done, var2_ps = sem("ysum_done"), sem("mean2_ps"), sem("v2_done"), sem("var2_ps")
        affine_done, vbias_done = sem("affine_done"), sem("vbias_done")
        x1n_dve, x1n_act = sem("x1n_dve"), sem("x1n_act")
        inA_ps, inB_ps, inA_done, inB_done = sem("inA_ps"), sem("inB_ps"), sem("inA_done"), sem("inB_done")
        toep_dve, toep_pool, toep_act = sem("toep_dve"), sem("toep_pool"), sem("toep_act")
        inU_done, stack_in, tap_step, stack_done, stack_back = (
            sem("inU_done"), sem("stack_in"), sem("tap_step"), sem("stack_done"), sem("stack_back"))
        moved_dve, moved_act = sem("moved_dve"), sem("moved_act")
        h0_twice = [sem("h0_twice_01"), sem("h0_twice_23")]
        p0_done, h1_hi_done, h1_lo_done = sem("p0_done"), sem("h1_hi_done"), sem("h1_lo_done")
        pw_hi_done, pw_lo_done = sem("pw_hi_done"), sem("pw_lo_done")
        h0_hi_done, h0_lo_done = sem("h0_hi_done"), sem("h0_lo_done")
        o_done, x1_pool, x1_biased = sem("o_done"), sem("x1_pool"), sem("x1_biased")
        cin_in = [sem(f"cin_in{g}") for g in range(NG)]
        conv_ps, conv_done = sem("conv_ps"), sem("conv_done")
        dw_in = [sem(f"dw_in{i}") for i in range(3)]
        h0_done, pw0_ps, h1_done, pw1_ps, h2_done, out_ps = (
            sem("h0_done"), sem("pw0_ps"), sem("h1_done"), sem("pw1_ps"), sem("h2_done"), sem("out_ps"))
        y_done = [sem("y_act"), sem("y_dve")]
        stored = sem("stored")
        dve_step = sem("dve_step")
        pads_done = sem("pads_done")

        x1n_need = []
        for k in range(NCH):
            upto = range((k + 1) * IPC)
            x1n_need.append((len([b for b in upto if b not in ACT_IMAGES]), len([b for b in upto if b in ACT_IMAGES])))

        def inner(t):
            return t[:, :, PAD:PAD + B * PITCH].rearrange("p h (b s) -> p b h s", s=PITCH)[:, :, :, 0:W]

        def pair(t, k):
            return t[:, :, k * IPC * W:(k + 1) * IPC * W]

        def channels(tile, first, g):
            (_, _, n, _, _), j = GROUPS[g]
            return tile[first + j:first + j + n * (GC - 1) + 1:n, :, :]

        def send_back(queue, g):
            stage, first = GROUPS[g][0][0:2]
            queue.dma_start(channels(dw[stage], first, g), cout[:, g % COUT, :]).then_inc(dw_in[stage], 16)

        def image(t, b):
            return t[:, :, b * W:(b + 1) * W]

        def last_out(b):
            i, at = ((4 + b // IPC, b % IPC * HW) if b < B // 2 else ((6, 7, 0, 1)[b - B // 2], 0))
            return bank[i][:, at:at + HW].rearrange("p (h w) -> p h w", h=H)

        def move_back(copy, k, done):
            copy(pair(dw[2][DVE_AT:C], k).rearrange("p h (b w) -> p b h w", w=W),
                 dwU[DVE_AT:C, k * IPC:(k + 1) * IPC]).then_inc(done, 1)

        def parts_of(k, s):
            return parts0[:, k].rearrange("p (h n) -> p h n", h=H) if s == 0 else pair(parts, k)

        def take_first_bits(k, s):
            return nc.scalar.copy(parts_of(k, s)[0:DIMS[s]], pair(dw[s][0:DIMS[s]], k))

        def take_last_bits(k, s):
            return nc.gpsimd.tensor_tensor(parts_of(k, s)[DIMS[s]:2 * DIMS[s]], pair(dw[s][0:DIMS[s]], k),
                                           parts_of(k, s)[0:DIMS[s]].bitcast(F32), ALU.subtract)

        def cout_free(eng, g):
            if g >= COUT:
                s = GROUPS[g - COUT][0][0]
                eng.wait_ge(dw_in[s], 16 * NGR[s])

        def wait_matrices(eng, q):
            for blocks, done in ((DVE_BLOCKS, toep_dve), (POOL_BLOCKS, toep_pool), (ACT_BLOCKS, toep_act)):
                if any(b[0] == q for b in blocks):
                    eng.wait_ge(done, 1 + max(i for i, b in enumerate(blocks) if b[0] == q))

        def matrices_at(q, c):
            at = slice(q * QUAD, (q + 1) * QUAD)
            return toep[:, at, :, c, :], taps_sb[:, at], ecol("blk")[:, c:c + 1]

        block = ctx.enter_context(nc.Block())

        @block.sync
        def _(sp):
            for k in range(NCH):
                sp.dma_start(x_sb[:, k * IPC:(k + 1) * IPC, :, :].rearrange("c b h w -> c b (h w)"),
                             x[k * IPC:(k + 1) * IPC].rearrange("b c h w -> c b (h w)")).then_inc(x_in[k], 16)
            sp.dma_start(e_sb[:, :], early).then_inc(early_in, 16)
            for s in range(3):
                sp.dma_start(taps_sb[:, G0[s]:G0[s] + NGR[s]], taps[:, G0[s]:G0[s] + NGR[s]]).then_inc(taps_in[s], 16)
            sp.dma_start(l_sb[:, :], late).then_inc(late_in, 16)
            sp.wait_ge(pads_done, 1)
            def send_stack(k):
                sp.wait_ge(inU_done, k + 1)
                sp.dma_start(stack[k:k + NCH * (DVE_CH - 1) + 1:NCH, :], abcU[DVE_AT:C, k, :]).then_inc(stack_in, 16)

            for k in range(NCH - 1):
                send_stack(k)
            for g in range(NG):
                tile, first = GROUPS[g][0][3:5]
                sp.wait_ge((inA_done, inB_done)[tile], NCH)
                sp.dma_start(cin[:, g, :], channels((abcA, abcB)[tile], first, g)).then_inc(cin_in[g], 16)
                if g == 0:
                    send_stack(NCH - 1)
            for g in range(G0[1], NG):
                if g == NG - 2:
                    sp.wait_ge(stack_done, 1)
                    sp.dma_start(dwU[DVE_AT:C].rearrange("p b h w -> p (b h w)"),
                                 summed[:, :, :].rearrange("p b n -> p (b n)")).then_inc(stack_back, 16)
                sp.wait_ge(conv_done, g + 1)
                send_back(sp, g)
                if g - H0_TWICE_AT in range(NCH // 2):
                    n = g - H0_TWICE_AT
                    sp.wait_ge(h0_lo_done, 2 * n + 2)
                    sp.dma_start(parts0[C // 2:C, 2 * n:2 * n + 2].bitcast(F32),
                                 parts0[0:C // 2, 2 * n:2 * n + 2].bitcast(F32)
                                 ).then_inc(h0_twice[n], 16)
            for first, end, done, n in [(0, 2, 0, 1), (2, 4, 0, 2), (4, 6, 1, 2), (6, 8, 1, 4)]:
                sp.wait_ge(y_done[done], n)
                sp.dma_start(out[first:end].rearrange("b c h w -> c b (h w)"),
                             x1[:, first:end].rearrange("c b h w -> c b (h w)")).then_inc(stored, 16)
            sp.wait_ge(stored, 16 * 4)

        @block.gpsimd
        def _(pool):
            for n, k in enumerate(POOL_CHUNKS):
                im, half = slice(k * IPC, (k + 1) * IPC), slice(n * IPC, (n + 1) * IPC)
                pool.wait_ge(x_in[k], 16)
                xs = x_sb[:, im].rearrange("p b h w -> p (b h w)").rearrange("p (n s) -> p n s", s=2)
                nc.gpsimd.tensor_tensor(pairs[:, half], xs[:, :, 0], xs[:, :, 1], ALU.add).then_inc(pairs_done, 1)
                pool.wait_ge(pairs_done, n + 1)
                ps = pairs[:, half].rearrange("p b n -> p (b n)").rearrange("p (n s) -> p n s", s=2)
                nc.gpsimd.tensor_tensor(colsum[:, im].rearrange("p b h v -> p (b h v)"), ps[:, :, 0], ps[:, :, 1],
                                        ALU.add).then_inc(colsum_pool, 1)
            nc.gpsimd.memset(abcA[:, :, :], 0.0)
            nc.gpsimd.memset(abcB[:, :, :], 0.0)
            nc.gpsimd.memset(abcU[:, :, :], 0.0).then_inc(pads_done, 1)
            pool.wait_ge(early_in, 16)

            for n, (q, c) in enumerate(POOL_BLOCKS):
                if n == POOL_RESIDUAL_AT:
                    pool.wait_ge(o_done, 1)
                    for k in POOL_RESIDUAL:
                        im = slice(k * IPC, (k + 1) * IPC)
                        nc.gpsimd.tensor_tensor(
                            x1[:, im].rearrange("p b h w -> p (b h) w"), x_sb[:, im].rearrange("p b h w -> p (b h) w"),
                            o_sb[:, im].rearrange("p b h -> p (b h)").unsqueeze(2).to_broadcast([C, IPC * H, W]),
                            ALU.add).then_inc(x1_pool, 1)
                pool.wait_ge(taps_in[1], 16)
                block_at, taps_at, mask = matrices_at(q, c)
                nc.gpsimd.tensor_scalar(block_at, taps_at, mask, 1.0, ALU.mult, ALU.mult).then_inc(toep_pool, 1)
            pool.wait_ge(pw_hi_done, 2)
            pool.wait_ge(toep_pool, len(POOL_BLOCKS))
            nc.gpsimd.tensor_tensor(pw0_parts[C // 2:C, :], lcol("pw0", C // 2), pw0_parts[0:C // 2, :].bitcast(F32),
                                    ALU.subtract).then_inc(pw_lo_done, 1)
            pool.wait_ge(pw_lo_done, 1)
            nc.gpsimd.tensor_tensor(pw1_lo[:, :], lcol("pw1"), pw1_hi[:, :].bitcast(F32), ALU.subtract
                                    ).then_inc(pw_lo_done, 1)
            for g in range(G0[1]):
                pool.wait_ge(conv_done, g + 1)
                send_back(pool, g)
            pool.wait_ge(dw_in[0], 16 * NGR[0])
            pool.wait_ge(inA_done, NCH)
            for k in range(NCH):
                at = pair(dw[0][0:DIMS[0]], k).rearrange("p h (b w) -> p b h w", w=W)
                nc.gpsimd.tensor_tensor(at, inner(abcA)[0:DIMS[0], k * IPC:(k + 1) * IPC], at, ALU.mult
                                        ).then_inc(h0_done, 1)
            pool.wait_ge(h0_done, NCH)
            for k in range(NCH):
                pool.wait_ge(h0_hi_done, k + 1)
                take_last_bits(k, 0).then_inc(h0_lo_done, 1)
            pool.wait_ge(h0_lo_done, NCH)
            pool.wait_ge(x1n_dve, B - len(ACT_IMAGES))
            pool.wait_ge(x1n_act, len(ACT_IMAGES))
            pool.wait_ge(x1_pool, len(POOL_RESIDUAL))
            for k in range(NCH):
                im = slice(k * IPC, (k + 1) * IPC)
                nc.gpsimd.tensor_scalar(x1[:, im], x1[:, im], ecol("b_out"), 1.0, ALU.add, ALU.mult
                                        ).then_inc(x1_biased, 1)
            pool.wait_ge(x1_biased, NCH)
            pool.wait_ge(dw_in[1], 16 * NGR[1])
            for k in range(NCH):
                pool.wait_ge(p0_done, k + 1)
                at = pair(dw[1][0:DIMS[1]], k)
                nc.gpsimd.tensor_tensor(at, p0[:, k], at, ALU.mult).then_inc(h1_done, 1)
            pool.wait_ge(h1_done, NCH)
            for k in range(NCH):
                pool.wait_ge(h1_hi_done, k + 1)
                take_last_bits(k, 1).then_inc(h1_lo_done, 1)

        @block.scalar
        def _(act):
            act.dma_start(g_sb[:, :], gavg).then_inc(gavg_in, 16)
            act.wait_ge(gavg_in, 16)
            nc.scalar.activation(warm[:, 0:1], g_sb[:, 0:1], ACT.Sqrt)
            act.wait_ge(early_in, 16)
            act.wait_ge(var_ps, 1)
            nc.scalar.activation(std[:, :], psV[:, 0:B], ACT.Sqrt, bias=ecol("eps")).then_inc(std_done, 1)
            nc.scalar.activation(warm[:, 1:2], g_sb[:, 0:1], ACT.Exp)
            act.wait_ge(qk_ps, 1)
            nc.scalar.activation(q_sb[:, :], psQ[:, 0:C], ACT.Identity, bias=ecol("bq")).then_inc(q_done, 1)
            act.wait_ge(score_done, 1)
            nc.scalar.activation(probs[:, :], score[:, :], ACT.Exp, bias=nmax[:, :], accum_out=rsum[:, :]
                                 ).then_inc(exp_done, 1)
            act.wait_ge(v_ps, 1)
            nc.scalar.copy(v_sb[:, :], psVt[:, 0:C]).then_inc(v_done, 1)
            nc.scalar.activation(warm[:, 2:3], g_sb[:, 0:1], ACT.Sqrt)
            act.wait_ge(taps_in[2], 16)

            todo = list(ACT_BLOCKS)

            def next_matrices():
                block_at, taps_at, mask = matrices_at(*todo.pop(0))
                nc.scalar.activation(block_at, taps_at, ACT.Copy, scale=mask).then_inc(toep_act, 1)

            for _ in range(ACT_HEAD):
                next_matrices()
            act.wait_ge(var2_ps, 1)
            nc.scalar.activation(std2[:, :], psV[:, 0:B], ACT.Sqrt, bias=ecol("eps"), scale=8.0 / (GN * HW)
                                 ).then_inc(std2_done, 1)
            act.wait_ge(affine_done, 1)
            for b in ACT_IMAGES:
                if b // IPC in POOL_RESIDUAL:
                    act.wait_ge(x1_pool, POOL_RESIDUAL.index(b // IPC) + 1)
                nc.scalar.activation(x1n[:, b, :], x1[:, b, :, :].rearrange("p h w -> p (h w)"), ACT.Identity,
                                     bias=b2[:, b:b + 1], scale=a2[:, b:b + 1]).then_inc(x1n_act, 1)
            act.wait_ge(pads_done, 1)
            for k in range(NCH):
                act.wait_ge(inA_ps, k + 1)
                nc.scalar.activation(inner(abcA)[0:DVE_AT, k * IPC:(k + 1) * IPC],
                                     bank[k][0:DVE_AT, :].rearrange("p (b h w) -> p b h w", b=IPC, h=H),
                                     ACT.Identity, bias=ecol("b_inA", DVE_AT)).then_inc(inA_done, 1)
            for k in range(NCH):
                act.wait_ge(inB_ps, k + 1)
                nc.scalar.activation(inner(abcB)[:, k * IPC:(k + 1) * IPC],
                                     bank[4 + k][:, :].rearrange("p (b h w) -> p b h w", b=IPC, h=H),
                                     ACT.Identity, bias=ecol("b_inB")).then_inc(inB_done, 1)
            nc.scalar.copy(pw0_parts[0:C // 2, :], lcol("pw0", C // 2)).then_inc(pw_hi_done, 1)
            nc.scalar.copy(pw1_hi[:, :], lcol("pw1")).then_inc(pw_hi_done, 1)
            act.wait_ge(inB_ps, NCH)
            for g in range(NG):
                cout_free(act, g)
                act.wait_ge(conv_ps, g + 1)
                nc.scalar.activation(cout[:, g % COUT, :], conv_bank[g % 3][:, 0:BW], ACT.Identity,
                                     bias=ecol("dw_b")[:, g:g + 1]).then_inc(conv_done, 1)
                if todo:
                    next_matrices()
                if g - H0_HI_AT in range(NCH):
                    k = g - H0_HI_AT
                    act.wait_ge(h0_done, k + 1)
                    take_first_bits(k, 0).then_inc(h0_hi_done, 1)
                if g - P0_AT in range(NCH // 2):
                    for k in (2 * (g - P0_AT), 2 * (g - P0_AT) + 1):
                        act.wait_ge(pw0_ps, k + 1)
                        nc.scalar.activation(p0[:, k], bank[k][0:DIMS[1], :].rearrange("p (h n) -> p h n", h=H),
                                             ACT.Identity, bias=ecol("pw0_b", DIMS[1])).then_inc(p0_done, 1)
                if g - H1_HI_AT in range(NCH):
                    k = g - H1_HI_AT
                    act.wait_ge(h1_done, k + 1)
                    take_first_bits(k, 1).then_inc(h1_hi_done, 1)
            act.wait_ge(stack_back, 16)
            for k in range(NCH):
                if k not in MOVED_BY_DVE:
                    move_back(nc.scalar.copy, k, moved_act)
            for k in range(NCH // 2):
                act.wait_ge(out_ps, (k + 1) * IPC)
                nc.scalar.copy(x1[:, k * IPC:(k + 1) * IPC].rearrange("p b h w -> p (b h w)"), bank[4 + k][:, :]
                               ).then_inc(y_done[0], 1)

        @block.vector
        def _(dve):
            steps = [0]

            def mark(ins):
                steps[0] += 1
                ins.then_inc(dve_step, 1)
                return steps[0]

            def link(ins):
                dve.wait_ge(dve_step, mark(ins))

            for k in range(NCH):
                dve.wait_ge(x_in[k], 16)
                for b in range(k * IPC, (k + 1) * IPC):
                    nc.vector.bn_stats(st[:, b, :], x_sb[:, b, :, :].rearrange("p h w -> p (h w)")
                                       ).then_inc(stats_done, 1)

            def column_sums(k):
                im = slice(k * IPC, (k + 1) * IPC)
                return nc.vector.tensor_reduce(
                    colsum[:, im], x_sb[:, im].rearrange("p b h (v s) -> p b h v s", s=S), AX_X, ALU.add)

            column_sums(2)
            dve.wait_ge(stats_done, B)
            dve.wait_ge(mean_ps, 1)
            link(nc.vector.tensor_tensor(dev[:, :, :], st[:, :, 1:6:3],
                                         psM[:, 0:B].unsqueeze(2).to_broadcast([C, B, 2]), ALU.subtract))
            link(nc.vector.tensor_tensor(dev2[:, :, :], dev[:, :, :], dev[:, :, :], ALU.mult))
            nc.vector.scalar_tensor_tensor(vpart[:, :, :], st[:, :, 2:6:3], 2.0 / HW, dev2[:, :, :],
                                           ALU.mult, ALU.add).then_inc(vpart_done, 1)
            dve.wait_ge(colsum_pool, len(POOL_CHUNKS))
            link(nc.vector.tensor_reduce(
                sums[:, 0, :, :], colsum[:, :, :, :].rearrange("p b (u s) v -> p (b u) v s", s=S), AX_X, ALU.add))

            def centre(half):
                return nc.vector.scalar_tensor_tensor(
                    centred[:, half, :, :], sums[:, half, :, :], 1.0 / H,
                    psM[:, 0:B].unsqueeze(2).to_broadcast([C, B, H]), ALU.mult, ALU.subtract)

            def normalise(half):
                nc.vector.tensor_tensor(normed[:, half, :, :], centred[:, half, :, :],
                                        a1[:, :].unsqueeze(2).to_broadcast([C, B, H]), ALU.mult
                                        ).then_inc(normed_done, 1)

            link(centre(0))
            dve.wait_ge(std_done, 1)
            link(nc.vector.reciprocal(a1[:, :], std[:, :]))
            normalise(0)
            link(nc.vector.tensor_reduce(sums[:, 1, :, :], colsum[:, :, :, :], AX_X, ALU.add))
            dve.wait_ge(early_in, 16)
            dve.wait_ge(qk_ps, 2)
            nc.vector.tensor_scalar(k_sb[:, :], psK[:, 0:C], ecol("bk"), None, ALU.add).then_inc(k_done, 1)
            link(centre(1))
            dve.wait_ge(score_ps, 1)
            link(nc.vector.scalar_tensor_tensor(score[:, :], psS[:, 0:C], float(C) ** -0.5, ecol("offmask"),
                                                ALU.mult, ALU.add))
            nc.vector.tensor_reduce(nmax[:, :], score[:, :], AX_X, ALU.max, negate=True).then_inc(score_done, 1)
            normalise(1)
            nc.vector.tensor_tensor(mdiff[:, :], st[:, :, 1], st[:, :, 4], ALU.subtract)
            nc.vector.tensor_tensor(msum[:, :], st[:, :, 1], st[:, :, 4], ALU.add)
            nc.vector.tensor_tensor(m2[:, :], st[:, :, 2], st[:, :, 5], ALU.add)
            nc.vector.tensor_scalar(vbias[:, :], ecol("bv"), float(W), None, ALU.mult).then_inc(vbias_done, 1)
            dve.wait_ge(exp_done, 1)
            link(nc.vector.reciprocal(rinv[:, :], rsum[:, :]))
            nc.vector.tensor_scalar(pnorm[:, :], probs[:, :], rinv[:, :], None, ALU.mult).then_inc(pnorm_done, 1)
            link(nc.vector.tensor_tensor(mdiff[:, :], mdiff[:, :], mdiff[:, :], ALU.mult))
            nc.vector.scalar_tensor_tensor(m2[:, :], mdiff[:, :], HW / 4.0, m2[:, :], ALU.mult, ALU.add)
            link(nc.vector.scalar_tensor_tensor(rcen[:, :, :], msum[:, :].unsqueeze(2).to_broadcast([C, B, H]),
                                                -W / 2.0, sums[:, 1, :, :], ALU.mult, ALU.add))
            dve.wait_ge(pT_ps, 1)
            nc.vector.tensor_copy(pT[:, :], psP[:, 0:C]).then_inc(pT_done, 1)
            squared = mark(nc.vector.tensor_tensor(rcen[:, :, :], rcen[:, :, :], rcen[:, :, :], ALU.mult))
            dve.wait_ge(vbias_done, 1)
            xrow_there = mark(nc.vector.tensor_scalar(xrow[:, :, :], sums[:, 1, :, :], 1.0 / W, vbias[:, :],
                                                      ALU.mult, ALU.add))
            dve.wait_ge(dve_step, squared)
            rsq_there = mark(nc.vector.tensor_reduce(rsq[:, :], rcen[:, :, :], AX_X, ALU.add))
            dve.wait_ge(o_ps, 1)
            dve.wait_ge(dve_step, xrow_there)
            yrow_there = mark(nc.vector.scalar_tensor_tensor(
                yrow[:, :, :].rearrange("p b h -> p (b h)"), psO[:, 0:C], float(W),
                xrow[:, :, :].rearrange("p b h -> p (b h)"), ALU.mult, ALU.add))
            dve.wait_ge(dve_step, rsq_there)
            within_there = mark(nc.vector.scalar_tensor_tensor(within[:, :], rsq[:, :], -1.0 / W, m2[:, :],
                                                               ALU.mult, ALU.add))
            dve.wait_ge(dve_step, yrow_there)
            nc.vector.tensor_reduce(ysum[:, :], yrow[:, :, :], AX_X, ALU.add).then_inc(ysum_done, 1)
            nc.vector.tensor_scalar(o_sb[:, :, :].rearrange("p b h -> p (b h)"), psO[:, 0:C], ecol("bv"),
                                    float(W), ALU.add, ALU.mult).then_inc(o_done, 1)
            dve.wait_ge(dve_step, within_there)
            nc.vector.tensor_scalar(within[:, :], within[:, :], 0.0, None, ALU.max)
            dve.wait_ge(o_done, 1)

            def residual(k):
                im = slice(k * IPC, (k + 1) * IPC)
                return nc.vector.tensor_tensor(
                    x1[:, im].rearrange("p b h w -> p (b h) w"), x_sb[:, im].rearrange("p b h w -> p (b h) w"),
                    o_sb[:, im].rearrange("p b h -> p (b h)").unsqueeze(2).to_broadcast([C, IPC * H, W]), ALU.add)

            dve.wait_ge(mean2_ps, 1)
            link(nc.vector.scalar_tensor_tensor(yd[:, :, :], psM[:, 0:B].unsqueeze(2).to_broadcast([C, B, H]),
                                                -8.0 / (GN * H), yrow[:, :, :], ALU.mult, ALU.add))
            link(nc.vector.tensor_tensor(yd2[:, :, :], yd[:, :, :], yd[:, :, :], ALU.mult))
            link(nc.vector.tensor_reduce(yq[:, :], yd2[:, :, :], AX_X, ALU.add))
            nc.vector.scalar_tensor_tensor(v2[:, :], yq[:, :], float(W), within[:, :], ALU.mult, ALU.add
                                           ).then_inc(v2_done, 1)
            nc.vector.tensor_scalar(mean2[:, :], psM[:, 0:B], 8.0 / (GN * H), None, ALU.mult)
            link(residual(0))
            dve.wait_ge(std2_done, 1)
            link(nc.vector.reciprocal(a2[:, :], std2[:, :]))
            for b in range(B):
                if b // IPC in POOL_RESIDUAL:
                    dve.wait_ge(x1_pool, POOL_RESIDUAL.index(b // IPC) + 1)
                if b not in ACT_IMAGES:
                    nc.vector.tensor_scalar(x1n[:, b, :], x1[:, b, :, :].rearrange("p h w -> p (h w)"),
                                            mean2[:, b:b + 1], a2[:, b:b + 1], ALU.subtract, ALU.mult
                                            ).then_inc(x1n_dve, 1)
                if b == 0:
                    nc.vector.scalar_tensor_tensor(b2[:, :], psM[:, 0:B], -8.0 / (GN * H), a2[:, :],
                                                   ALU.mult, ALU.mult).then_inc(affine_done, 1)
            dve.wait_ge(pads_done, 1)
            for k in range(NCH):
                dve.wait_ge(inA_ps, k + 1)
                at = abcU[DVE_AT:C, k, PAD + PAD * PITCH:PAD + PAD * PITCH + W]
                at = bass.AP(at.tensor, at.offset, [at.ap[0], [(H + PAD) * PITCH, IPC], [PITCH, H], [1, W]])
                nc.vector.tensor_scalar(at, bank[k][DVE_AT:C, :].rearrange("p (b h w) -> p b h w", b=IPC, h=H),
                                        ecol("b_inA")[DVE_AT:C], None, ALU.add).then_inc(inU_done, 1)
            for q, c in DVE_BLOCKS:
                dve.wait_ge(taps_in[0 if q == 0 else 2], 16)
                block_at, taps_at, mask = matrices_at(q, c)
                nc.vector.tensor_scalar(block_at, taps_at, mask, None, ALU.mult).then_inc(toep_dve, 1)
            dve.wait_ge(late_in, 16)
            dve.wait_ge(stack_in, NCH * 16)
            for n in range(K * K):
                at = stack[:, n // K * PITCH + n % K:n // K * PITCH + n % K + 1]
                src = bass.AP(at.tensor, at.offset, [at.ap[0], [PITCH, ROWS], [1, W]])
                dst = acc[:, n % ACCS, :, :]
                tap = lcol("dve_taps")[:, n:n + 1]
                if n == 0:
                    ins = nc.vector.tensor_scalar(dst, src, tap, lcol("dve_bias"), ALU.mult, ALU.add)
                elif n < ACCS:
                    ins = nc.vector.tensor_scalar(dst, src, tap, None, ALU.mult)
                else:
                    if (n - ACCS) % (ACCS - 1) == 0:
                        dve.wait_ge(tap_step, n - 1)
                    ins = nc.vector.scalar_tensor_tensor(dst, src, tap, dst, ALU.mult, ALU.add)
                ins.then_inc(tap_step, 1)
            dve.wait_ge(tap_step, K * K)
            halves = []
            for n in range(ACCS):
                at = acc[:, n, 0, :]
                halves.append(bass.AP(at.tensor, at.offset, [at.ap[0], [(H + PAD) * W, IPC], [1, HW]]))
            nc.vector.tensor_tensor(summed[:, :, :], halves[0], halves[1], ALU.add).then_inc(stack_done, 1)
            dve.wait_ge(stack_back, 16)
            for k in MOVED_BY_DVE:
                move_back(nc.vector.tensor_copy, k, moved_dve)
            dve.wait_ge(dw_in[2], 16 * NGR[2])
            dve.wait_ge(moved_dve, len(MOVED_BY_DVE))
            for b in range(B):
                if b // IPC not in MOVED_BY_DVE:
                    dve.wait_ge(moved_act, NCH - len(MOVED_BY_DVE))
                dve.wait_ge(pw1_ps, b // IPC + 1)
                nc.vector.scalar_tensor_tensor(
                    image(dw[2], b), image(bank[b // IPC][:, :].rearrange("p (h n) -> p h n", h=H), b % IPC),
                    ecol("pw1_b"), image(dw[2], b), ALU.add, ALU.mult).then_inc(h2_done, 1)
            dve.wait_ge(x1_biased, NCH)
            for b in range(B // 2, B):
                dve.wait_ge(out_ps, b + 1)
                nc.vector.tensor_tensor(x1[:, b], x1[:, b], last_out(b), ALU.add).then_inc(y_done[1], 1)

        @block.tensor
        def _(pe):
            mm = nc.tensor.matmul
            gavg = g_sb[:, :]

            def keep_warm(n):
                for _ in range(n):
                    mm(unread[:, 0:C], gavg, gavg, start=True, stop=True)

            pe.wait_ge(gavg_in, 16)
            keep_warm(WARM[0])
            pe.wait_ge(stats_done, B)
            mm(psM[:, 0:B], gavg, st[:, :, 1], start=True, stop=False)
            mm(psM[:, 0:B], gavg, st[:, :, 4], start=False, stop=True).then_inc(mean_ps, 1)
            keep_warm(WARM[1])
            pe.wait_ge(vpart_done, 1)
            mm(psV[:, 0:B], gavg, vpart[:, :, 0], start=True, stop=False)
            mm(psV[:, 0:B], gavg, vpart[:, :, 1], start=False, stop=True).then_inc(var_ps, 1)
            keep_warm(WARM[2])
            pe.wait_ge(early_in, 16)
            pe.wait_ge(normed_done, 1)
            mm(psQ[:, 0:C], ecol("wq"), normed[:, 0, :, :], start=True, stop=True).then_inc(qk_ps, 1)
            mm(psK[:, 0:C], ecol("wk"), normed[:, 0, :, :], start=True, stop=True).then_inc(qk_ps, 1)
            pe.wait_ge(q_done, 1)
            pe.wait_ge(k_done, 1)
            mm(psS[:, 0:C], q_sb[:, :], k_sb[:, :], start=True, stop=True).then_inc(score_ps, 1)
            keep_warm(WARM[3])
            pe.wait_ge(normed_done, 2)
            mm(psVt[:, 0:C], normed[:, 1, :, :], ecol("wv"), start=True, stop=True).then_inc(v_ps, 1)
            keep_warm(WARM[4])
            pe.wait_ge(pnorm_done, 1)
            nc.tensor.transpose(psP[:, 0:C], pnorm[:, :], ecol("ident")).then_inc(pT_ps, 1)
            pe.wait_ge(pT_done, 1)
            pe.wait_ge(v_done, 1)
            mm(psO[:, 0:C], v_sb[:, :], pT[:, :], start=True, stop=True).then_inc(o_ps, 1)
            keep_warm(WARM[5])
            pe.wait_ge(ysum_done, 1)
            mm(psM[:, 0:B], gavg, ysum[:, :], start=True, stop=True).then_inc(mean2_ps, 1)
            keep_warm(WARM[6])
            pe.wait_ge(v2_done, 1)
            mm(psV[:, 0:B], gavg, v2[:, :], start=True, stop=True).then_inc(var2_ps, 1)
            keep_warm(WARM[7])
            pe.wait_ge(late_in, 16)
            for b in range(IPC):
                pe.wait_ge(x1n_dve, b + 1)
                ins = mm(bank[0][:, b * HW:(b + 1) * HW], lcol("w_in")[:, 0:C], x1n[:, b, :], start=True, stop=True)
            ins.then_inc(inA_ps, 1)
            for k in range(1, NCH):
                pe.wait_ge(x1n_dve, x1n_need[k][0])
                pe.wait_ge(x1n_act, x1n_need[k][1])
                mm(bank[k][:, :], lcol("w_in")[:, 0:C], x1n[:, k * IPC:(k + 1) * IPC, :], start=True, stop=True
                   ).then_inc(inA_ps, 1)
            for k in range(NCH):
                mm(bank[4 + k][:, :], lcol("w_in")[:, C:2 * C], x1n[:, k * IPC:(k + 1) * IPC, :],
                   start=True, stop=True).then_inc(inB_ps, 1)
            for g in range(NG):
                pe.wait_ge(cin_in[g], 16)
                if g % QUAD == 0:
                    wait_matrices(pe, g // QUAD)
                if g < 3:
                    pe.wait_ge(inB_done, g + 1)
                else:
                    pe.wait_ge(conv_done, g - 2)
                for kx in range(K):
                    rows = cin[:, g, 0:ROW - ROW % PITCH].rearrange("p (b s) -> p b s", s=PITCH)
                    src = bass.AP(rows.tensor, rows.offset + kx, [rows.ap[0], [PITCH, B], [1, W]])
                    last = mm(conv_bank[g % 3][:, 0:BW], toep[:, g, kx, :, :], src,
                              start=(kx == 0), stop=(kx == K - 1))
                last.then_inc(conv_ps, 1)
                if g == PW0_AFTER:
                    pe.wait_ge(pw_lo_done, 2)
                    for k in range(NCH):
                        pe.wait_ge(h0_twice[k // 2], 16)
                        mm(bank[k][0:DIMS[1], :], pw0_parts[:, :], parts0[:, k], start=True, stop=True
                           ).then_inc(pw0_ps, 1)
            for k in range(NCH):
                pe.wait_ge(h1_lo_done, k + 1)
                mm(bank[k][:, :], pw1_lo[:, :], pair(parts, k), start=True, stop=False)
                mm(bank[k][:, :], pw1_hi[:, :], pair(parts, k), start=False, stop=True).then_inc(pw1_ps, 1)
            pe.wait_ge(conv_done, NG)
            pe.wait_ge(x1_biased, NCH)
            for k in range(NCH // 2):
                mm(bank[4 + k][:, :], ecol("ident"), x1[:, k * IPC:(k + 1) * IPC].rearrange("p b h w -> p (b h w)"),
                   start=True, stop=False)
            for b in range(B):
                pe.wait_ge(h2_done, b + 1)
                mm(last_out(b), lcol("w_out"), image(dw[2], b), start=(b >= B // 2),
                   stop=(b >= B // 2 or b % IPC == IPC - 1)).then_inc(out_ps, 1)


def kernel(**inputs):
    import numpy as np
    import concourse.bacc as bacc
    from concourse.bass_utils import run_bass_kernel_spmd

    a = {k: np.ascontiguousarray(v) for k, v in inputs.items()}
    L0 = {k[8:]: v for k, v in a.items() if k.startswith("L0_conv_")}
    L1 = {k[8:]: v for k, v in a.items() if k.startswith("L1_conv_")}

    p = np.arange(C)
    same_group = (p[:, None] // GN == p[None, :] // GN)
    same_image = (p[:, None] // H == p[None, :] // H)
    early = np.zeros((C, E_N), np.float32)
    late = np.zeros((C, L_N), np.float32)

    def put(pack, cols, name, block):
        lo, hi = cols[name]
        pack[:block.shape[0], lo:lo + block.shape[1]] = block

    gavg = np.where(same_group, np.float32(1 / 8), np.float32(0))
    put(early, E_COL, "eps", np.full((C, 1), EPS, np.float32))
    put(early, E_COL, "ident", np.eye(C, dtype=np.float32))
    put(early, E_COL, "offmask", np.where(same_image, np.float32(0), np.float32(OFF_BLOCK)))
    put(early, E_COL, "blk", (p[:, None] // H == np.arange(GC)[None, :]).astype(np.float32))
    in_order = np.concatenate([np.arange(0, DVE_AT), np.arange(2 * C - DVE_CH, 2 * C),
                               np.arange(DVE_AT, 2 * C - DVE_CH)])
    w_in, b_in = L1["w_in"][in_order], L1["b_in"][in_order]
    for name, w in (("wq", L0["Wq"]), ("wk", L0["Wk"]), ("wv", L0["Wv"])):
        put(early, E_COL, name, w.T)
    for name, v in (("bq", L0["bq"]), ("bk", L0["bk"]), ("bv", L0["bv"]), ("b_inA", b_in[:C]),
                    ("b_inB", b_in[C:]), ("pw0_b", L1["pw0_b"]), ("pw1_b", L1["pw1_b"]),
                    ("b_out", L1["b_out"])):
        put(early, E_COL, name, v[:, None])
    for name, w in (("w_in", w_in), ("pw0", np.concatenate([L1["pw0_w"]] * 2, axis=1)), ("pw1", np.concatenate([L1["pw1_w"]] * 2, axis=1)), ("w_out", L1["w_out"])):
        put(late, L_COL, name, w.T)
    lo = E_COL["dw_b"][0]
    taps = np.zeros((GC, H, NG, K, H), np.float32)
    for g, ((stage, first, n, _, _), j) in enumerate(GROUPS):
        chan = sum(DIMS[:stage]) + first + j + n * np.arange(GC)
        early[:, lo + g] = np.repeat(L1["dw_b"][chan], H)
        for row_out in range(H):
            for row_in in range(max(0, row_out - PAD), min(H, row_out + PAD + 1)):
                taps[:, row_in, g, :, row_out] = L1["dw_w"][chan, 0, row_in - row_out + PAD, :]
    taps = taps.reshape(C, NG, K, H)
    first = sum(DIMS[:2]) + DVE_AT
    put(late, L_COL, "dve_taps", np.repeat(L1["dw_w"][first:first + DVE_CH, 0].reshape(DVE_CH, K * K), NCH, axis=0))
    put(late, L_COL, "dve_bias", np.repeat(L1["dw_b"][first:first + DVE_CH, None], NCH, axis=0))

    arrays = {"x": a["x"], "gavg": gavg, "early": early, "late": late, "taps": taps}
    nc = bacc.Bacc("TRN2", target_bir_lowering=False, num_devices=1)
    args = [nc.dram_tensor(f"in_{n}", v.shape, F32, kind="ExternalInput").ap() for n, v in arrays.items()]
    out = nc.dram_tensor("out_0", (B, C, H, W), F32, kind="ExternalOutput").ap()
    build(nc, *args, out)
    r = run_bass_kernel_spmd(nc, [{f"in_{n}": v for n, v in arrays.items()}], core_ids=[0])
    return r.results[0]["out_0"]
```
